# Optimizing a Trainium2 kernel written in Bass

```python
import numpy as np
import jax
import jax.numpy as jnp

def _softmax(x, axis=-1):
    return jax.nn.softmax(x, axis=axis)

def _gelu(x):
    return jax.nn.gelu(x, approximate=True)

def _silu(x):
    return jax.nn.silu(x)

def _sigmoid(x):
    return jax.nn.sigmoid(x)

def _layernorm(x, axis=-1, eps=1e-05):
    m = jnp.mean(x, axis=axis, keepdims=True)
    v = jnp.var(x, axis=axis, keepdims=True)
    return (x - m) / jnp.sqrt(v + eps)

def _scatter_add(tgt, idx, src, axis=0):
    return tgt.at[idx].add(src)

def _segment_sum(src, seg, n):
    return jax.ops.segment_sum(src, seg, n)
kernel_name = 'mk_seq_preln_d1_jaxref_r4_826e3a'

def setup_inputs(seed: int=0):
    np.random.seed(seed)
    _w = jnp.asarray

    def _L0_attn_setup():
        import jax, jax.numpy as jnp
        import numpy as np
        import math
        B, N, E, D = (4, 2048, 256, 64)
        key = jax.random.key(seed)
        kx, kq, kk, kv, ko = jax.random.split(key, 5)
        x = jax.random.normal(kx, (B, N, E), dtype=jnp.float32)
        wq = jnp.sign(jax.random.normal(kq, (D, E), dtype=jnp.float32)) / math.sqrt(E)
        wk = jnp.sign(jax.random.normal(kk, (D, E), dtype=jnp.float32)) / math.sqrt(E)
        wv = jnp.sign(jax.random.normal(kv, (D, E), dtype=jnp.float32)) / math.sqrt(E)
        wo = jnp.sign(jax.random.normal(ko, (E, D), dtype=jnp.float32)) / math.sqrt(D)
        return {'x': x, 'wq': wq, 'wk': wk, 'wv': wv, 'wo': wo}
    _L0_attn_in = _L0_attn_setup()

    def _L0_ffn_setup():
        import jax, jax.numpy as jnp
        import numpy as np
        import math
        BETA = 0.9
        THRESHOLD = 1.0
        NUM_STEPS = 5
        ALPHA = 2.0

        @jax.custom_vjp
        def spike_fn(u):
            return (u > 0).astype(u.dtype)

        def _spike_fwd(u):
            return (spike_fn(u), u)

        def _spike_bwd(u, g):
            s = jnp.pi / 2.0 * ALPHA * u
            return (g * (ALPHA / 2.0) / (1.0 + s * s),)
        spike_fn.defvjp(_spike_fwd, _spike_bwd)
        key = jax.random.key(seed)
        k1, k2, k3 = jax.random.split(key, 3)
        n_embd = 256
        x = jax.random.normal(k1, (4, 512, n_embd), dtype=jnp.float32)
        W_fc = jax.random.normal(k2, (4 * n_embd, n_embd), dtype=jnp.float32) / math.sqrt(n_embd)
        W_proj = jax.random.normal(k3, (n_embd, 4 * n_embd), dtype=jnp.float32) / math.sqrt(4 * n_embd)
        return {'x': x, 'W_fc': W_fc, 'W_proj': W_proj}
    _L0_ffn_in = _L0_ffn_setup()
    _d = {'L0_attn_x': _L0_attn_in['x'], 'L0_attn_wq': _L0_attn_in['wq'], 'L0_attn_wk': _L0_attn_in['wk'], 'L0_attn_wv': _L0_attn_in['wv'], 'L0_attn_wo': _L0_attn_in['wo'], 'L0_ffn_W_fc': _L0_ffn_in['W_fc'], 'L0_ffn_W_proj': _L0_ffn_in['W_proj']}
    _x0 = _d['L0_attn_x']
    _d['L0_attn_x'] = jax.random.normal(jax.random.fold_in(jax.random.key(seed), 1), (8, 1024, 256), dtype=_x0.dtype)
    del _x0
    return _d

def reference(L0_attn_x, L0_attn_wq, L0_attn_wk, L0_attn_wv, L0_attn_wo, L0_ffn_W_fc, L0_ffn_W_proj):

    def _L0_attn_ref(x, wq, wk, wv, wo):
        import jax, jax.numpy as jnp
        import numpy as np
        import math
        B, N, E, D = (4, 2048, 256, 64)
        Q = jnp.einsum('bne,de->bnd', x, wq)
        K = jnp.einsum('bne,de->bnd', x, wk)
        V = jnp.einsum('bne,de->bnd', x, wv)
        energy = jnp.einsum('bnd,bne->bde', K, V)
        context = jnp.einsum('bnd,bde->bne', Q, energy)
        context = context * jnp.asarray(math.sqrt(3.0 / D), dtype=context.dtype)
        out = jnp.einsum('bnd,ed->bne', context, wo)
        return out

    def _L0_ffn_ref(x, W_fc, W_proj):
        import jax, jax.numpy as jnp
        import numpy as np
        import math
        BETA = 0.9
        THRESHOLD = 1.0
        NUM_STEPS = 5
        ALPHA = 2.0

        @jax.custom_vjp
        def spike_fn(u):
            return (u > 0).astype(u.dtype)

        def _spike_fwd(u):
            return (spike_fn(u), u)

        def _spike_bwd(u, g):
            s = jnp.pi / 2.0 * ALPHA * u
            return (g * (ALPHA / 2.0) / (1.0 + s * s),)
        spike_fn.defvjp(_spike_fwd, _spike_bwd)
        h = jnp.square(jax.nn.relu(jnp.einsum('bsd,fd->bsf', x, W_fc)))
        y = jnp.einsum('bsf,df->bsd', h, W_proj)

        def step(mem, _):
            reset = jax.lax.stop_gradient(spike_fn(mem - THRESHOLD))
            mem_new = BETA * mem + y - reset * THRESHOLD
            spk = spike_fn(mem_new - THRESHOLD)
            return (mem_new, spk)
        mem0 = jnp.zeros_like(y)
        _, spks = jax.lax.scan(step, mem0, None, length=NUM_STEPS)
        return jnp.sum(spks, axis=0) / NUM_STEPS
    x = L0_attn_x
    x = x + _L0_attn_ref(_layernorm(x, axis=-1), L0_attn_wq, L0_attn_wk, L0_attn_wv, L0_attn_wo)
    x = x + _L0_ffn_ref(_layernorm(x, axis=-1), L0_ffn_W_fc, L0_ffn_W_proj)
    return x

_drawn_inputs = setup_inputs


def setup_inputs(seed=0):
    import zlib

    import numpy as np

    out = dict(_drawn_inputs(seed))
    spreads = {}
    factors = {}
    for name, (base, spread) in spreads.items():
        noise = np.random.default_rng([zlib.crc32(name.encode()), seed]).standard_normal(out[name].shape)
        drawn = base * np.exp(spread * noise) if base else spread * noise
        out[name] = jnp.asarray(drawn.astype(out[name].dtype))
    for name, factor in factors.items():
        out[name] = (out[name] * factor).astype(out[name].dtype)
    return out
```

```python
import concourse.bass as bass
from concourse import mybir
from contextlib import ExitStack
import math
import numpy as np


BATCHES, SEQ, EMB, HEAD, HID = 8, 1024, 256, 64, 1024
P = 128
GROUP = 512
TILES = GROUP // P
GROUPS = BATCHES * SEQ // GROUP
PER_BATCH = SEQ // GROUP
EC = EMB // P
FC = HID // P
GE = TILES * EMB
RING = 4
EPS = 1e-5
ATT_SCALE = math.sqrt(3.0 / HEAD)
BETA, THRESHOLD, NUM_STEPS = 0.9, 1.0, 5
UNROLL = 4
FIRST = 1
LOOPS = (GROUPS - 3 - FIRST) // UNROLL
LAST = FIRST + UNROLL * LOOPS


def spike_counts(y):
    y, one = np.float32(y), np.float32(1.0)
    mem, count = np.float32(0.0), 0
    for _ in range(NUM_STEPS):
        reset = one if mem > np.float32(THRESHOLD) else np.float32(0.0)
        mem = np.float32(np.float32(np.float32(BETA) * mem) + y) - reset * np.float32(THRESHOLD)
        count += int(mem > np.float32(THRESHOLD))
    return count


def spike_thresholds():
    found = []
    for n in range(1, NUM_STEPS + 1):
        low, high = (int(np.float32(v).view(np.int32)) for v in (0.01, 4.0))
        while high - low > 1:
            mid = (low + high) // 2
            if spike_counts(np.int32(mid).view(np.float32)) >= n:
                high = mid
            else:
                low = mid
        found.append(float(np.int32(low).view(np.float32)))
    return found


def build(nc, x, w_kv, w_q, w_o, w_up, w_down, out):
    f32, f32r = mybir.dt.float32, mybir.dt.float32r
    ACT, ALU = mybir.ActivationFunctionType, mybir.AluOpType
    THETA = spike_thresholds()
    x_d = x.rearrange("(g p t) e -> g p (t e)", p=P, t=TILES)
    out_d = out.rearrange("(g p t) e -> g p (t e)", p=P, t=TILES)

    with ExitStack() as ctx:
        def sb(name, shape, dt=f32):
            return ctx.enter_context(nc.sbuf_tensor(name, shape, dt))

        def bank(name):
            return ctx.enter_context(nc.psum_tensor(name, [P, 512], f32))

        def sem(name):
            return ctx.enter_context(nc.semaphore(name))

        wkv_raw = sb("wkv_raw", [P, EC * 2 * HEAD])
        wq2 = sb("wq2", [P, EMB])
        wo2 = sb("wo2", [P, EMB])
        wkv_h, wkv_l = (sb(f"wkv_{s}", [P, EC, 2 * HEAD], f32r) for s in "hl")
        wup_h, wup_l = (sb(f"wup_{s}", [P, EC, HID], f32r) for s in "hl")
        wdn_h, wdn_l = (sb(f"wdn_{s}", [P, FC, EMB], f32r) for s in "hl")
        ident = sb("ident", [P, P])
        xs = sb("xs", [P, RING, GE])
        x1 = sb("x1", [P, RING, GE])
        xn = sb("xn", [P, GE])
        x2n = sb("x2n", [P, GE])
        xnT_h, xnT_l = (sb(f"xnT_{s}", [P, 2, EC, GROUP], f32r) for s in "hl")
        x2T_h, x2T_l = (sb(f"x2T_{s}", [P, 2, EC, GROUP], f32r) for s in "hl")
        kv = sb("kv", [P, TILES, 2, 2, HEAD], f32r)
        energy = sb("energy", [P, P])
        eo = sb("eo", [P, EMB])
        mix_h, mix_l = (sb(f"mix_{s}", [P, EC, EMB], f32r) for s in "hl")
        relu = sb("relu", [P, 2, GROUP])
        hid = sb("hid", [P, 4, GROUP])
        hid_h, hid_l = (sb(f"hid_{s}", [P, 2, FC, GROUP], f32r) for s in "hl")
        wup_raw = x1[:, 2:4, :].rearrange("p s n -> p (s n)")
        wdn_raw = hid[:, :, :].rearrange("p s n -> p (s n)")
        cnt = sb("cnt", [P, 2, 2, EMB])
        credit = sb("credit", [P, 1 + RING + 2])
        stat = [sb(f"stat{n}", [P, TILES, 6]) for n in (1, 2)]
        mv = [sb(f"mv{n}", [P, TILES, 2]) for n in (1, 2)]
        ve = [sb(f"ve{n}", [P, TILES]) for n in (1, 2)]
        rstd = [sb(f"rstd{n}", [P, TILES]) for n in (1, 2)]
        neg_half = sb("neg_half", [P, TILES])
        eps = sb("eps", [P, TILES])

        hid_ps = [bank(f"hid_ps{n}") for n in range(2)]
        y_ps = [bank(f"y_ps{n}") for n in range(2)]
        work_ps = [bank(f"work_ps{n}") for n in range(2)]
        kv_ps = bank("kv_ps")
        e_ps = bank("e_ps")

        x_loaded = [sem(f"x_loaded{n}") for n in range(RING)]
        x1_free = [sem(f"x1_free{n}") for n in range(RING)]
        w_loaded = {n: sem(f"w_loaded_{n}") for n in ("kv", "q", "o", "up", "down")}
        ident_zero, ident_ready, half_ready = sem("ident_zero"), sem("ident_ready"), sem("half_ready")
        wkv_high, wkv_ready = sem("wkv_high"), sem("wkv_ready")
        wff_high, wff_ready = sem("wff_high"), sem("wff_ready")
        stats_done = [sem(f"stats{n}_done") for n in (1, 2)]
        moments_ready = [sem(f"moments{n}_ready") for n in (1, 2)]
        ve_ready = [sem(f"ve{n}_ready") for n in (1, 2)]
        rstd_ready = [sem(f"rstd{n}_ready") for n in (1, 2)]
        xn_ready, x2n_ready = sem("xn_ready"), sem("x2n_ready")
        xn_turned, x2n_turned = sem("xn_turned"), sem("x2n_turned")
        xnT_high, xnT_ready = sem("xnT_high"), sem("xnT_ready")
        x2T_high, x2T_ready = sem("x2T_high"), sem("x2T_ready")
        kv_done, kv_high, kv_ready = sem("kv_done"), sem("kv_high"), sem("kv_ready")
        energy_done, energy_ready = sem("energy_done"), sem("energy_ready")
        eo_done, eo_ready = sem("eo_done"), sem("eo_ready")
        mix_done, mix_high, mix_ready = sem("mix_done"), sem("mix_high"), sem("mix_ready")
        att_done, x1_ready = sem("att_done"), sem("x1_ready")
        up_done, relu_done, hid_done = sem("up_done"), sem("relu_done"), sem("hid_done")
        hid_high, hid_ready = sem("hid_high"), sem("hid_ready")
        y_done, count_step, out_ready = sem("y_done"), sem("count_step"), sem("out_ready")
        y_free = sem("y_free")

        def wait(eng, s, r, value):
            first, per_loop = value
            if isinstance(r, int) and first + per_loop * r <= 0:
                return
            assert first > 0, (s, value)
            eng.wait_ge(s, r * per_loop + first)

        def upto(n, per=1, plus=0):
            return per * n + plus, per * UNROLL

        def upto_batches(n):
            return n // PER_BATCH, UNROLL // PER_BATCH

        def upto_slot(n, before=0):
            return 16 * (n // RING + 1 + before), 16 * UNROLL // RING

        def steps(eng, step):
            for i in range(-3, FIRST):
                step(0, i)
            with eng.Fori(0, LOOPS) as r:
                for j in range(UNROLL):
                    step(r, FIRST + j)
            for i in range(LAST, GROUPS + 1):
                step(0, i)

        def there(r, n):
            return not isinstance(r, int) or 0 <= n < GROUPS

        def closes_batch(n):
            return n % PER_BATCH == PER_BATCH - 1

        block = ctx.enter_context(nc.Block())

        @block.sync
        def _(sp):
            def load(r, n):
                wait(sp, x1_ready, r, upto(n - RING + 1))
                sp.dma_start(xs[:, n % RING, :], x_d[r * UNROLL + n, :, :]).then_inc(x_loaded[n % RING], 16)

            def store(r, n):
                wait(sp, out_ready, r, upto(n + 1, 2))
                sp.dma_start(out_d[r * UNROLL + n, :, :], x1[:, n % RING, :]).then_inc(x1_free[n % RING], 16)

            def step(r, i):
                if there(r, i + RING + 1):
                    load(r, i + RING + 1)
                if there(r, i - 1):
                    store(r, i - 1)

            load(0, 0)
            sp.dma_start(wkv_raw[:, :], w_kv).then_inc(w_loaded["kv"], 16)
            load(0, 1)
            sp.dma_start(wo2[:, :], w_o).then_inc(w_loaded["o"], 16)
            sp.dma_start(wq2[:, :], w_q).then_inc(w_loaded["q"], 16)
            sp.dma_start(wup_raw, w_up).then_inc(w_loaded["up"], 16)
            load(0, 2)
            sp.dma_start(wdn_raw, w_down).then_inc(w_loaded["down"], 16)
            load(0, 3)
            for i in range(-1, FIRST):
                step(0, i)
            loops = (GROUPS - RING - 1 - FIRST) // UNROLL
            with sp.Fori(0, loops) as r:
                for j in range(UNROLL):
                    step(r, FIRST + j)
            for i in range(FIRST + UNROLL * loops, GROUPS + 1):
                step(0, i)
            for s in x1_free:
                sp.wait_ge(s, 16 * (GROUPS // RING + 1))

        @block.gpsimd
        def _(pool):
            nc.gpsimd.memset(ident[:, :], 0.0).then_inc(ident_zero, 1)
            nc.gpsimd.memset(neg_half[:, :], -0.5).then_inc(half_ready, 1)
            nc.gpsimd.memset(eps[:, :], EPS).then_inc(half_ready, 1)
            pool.wait_ge(ident_zero, 1)
            nc.gpsimd.affine_select(out=ident[:, :], in_=ident[:, :], compare_op=ALU.not_equal, fill=1.0, base=0,
                                    pattern=[[-1, P]], channel_multiplier=1).then_inc(ident_ready, 1)
            pool.wait_ge(half_ready, 2)

            def inverse_deviation(r, n, which):
                wait(pool, moments_ready[which], r, upto(n + 1))
                wait(pool, (xn_ready, x2n_ready)[which], r, upto(n))
                nc.gpsimd.tensor_tensor(ve[which][:, :], mv[which][:, :, 1], eps[:, :], ALU.add)\
                    .then_inc(ve_ready[which], 1)
                wait(pool, ve_ready[which], r, upto(n + 1))
                nc.gpsimd.tensor_tensor(rstd[which][:, :], ve[which][:, :], neg_half[:, :], ALU.pow)\
                    .then_inc(rstd_ready[which], 1)

            def low_half(r, i, c):
                wait(pool, hid_high, r, upto(i, FC, c + 1))
                nc.gpsimd.tensor_tensor(hid_l[:, i % 2, c, :], hid[:, c % 4, :], hid_h[:, i % 2, c, :].bitcast(f32),
                                        ALU.subtract).then_inc(hid_ready, 1)

            def step(r, i):
                for c in range(FC):
                    if c == 3 and there(r, i + 3):
                        inverse_deviation(r, i + 3, 0)
                    if c == 5 and there(r, i + 1):
                        inverse_deviation(r, i + 1, 1)
                    if there(r, i):
                        low_half(r, i, c)

            steps(pool, step)

        @block.scalar
        def _(act):
            act.wait_ge(w_loaded["kv"], 16)
            nc.scalar.activation(wkv_h[:, :, :], wkv_raw[:, :], ACT.Copy).then_inc(wkv_high, 1)

            def feed_forward_weights():
                act.wait_ge(w_loaded["up"], 16)
                nc.scalar.activation(wup_h[:, :, :], wup_raw, ACT.Copy).then_inc(wff_high, 1)
                act.wait_ge(w_loaded["down"], 16)
                nc.scalar.activation(wdn_h[:, :, :], wdn_raw, ACT.Copy).then_inc(wff_high, 1)

            def rectify(r, i, c):
                wait(act, up_done, r, upto(i, FC, c + 1))
                wait(act, hid_done, r, upto(i, FC, c - 1))
                nc.scalar.activation(relu[:, c % 2, :], hid_ps[c % 2][:, :], ACT.Relu).then_inc(relu_done, 1)

            def square(r, i, c):
                wait(act, relu_done, r, upto(i, FC, c + 1))
                wait(act, hid_ready, r, upto(i, FC, c - 3))
                nc.scalar.activation(hid[:, c % 4, :], relu[:, c % 2, :], ACT.Square).then_inc(hid_done, 1)

            def high_half(r, i, c):
                wait(act, hid_done, r, upto(i, FC, c + 1))
                nc.scalar.activation(hid_h[:, i % 2, c, :], hid[:, c % 4, :], ACT.Copy).then_inc(hid_high, 1)

            def kv_high_half(r, n):
                wait(act, kv_done, r, upto(n + 1))
                wait(act, energy_done, r, upto(n))
                src = kv_ps[:, :].rearrange("p (a d) -> p a d", d=HEAD)
                dst = kv[:, :, :, 0, :].rearrange("p t s d -> p (t s) d")
                nc.scalar.activation(dst, src, ACT.Copy).then_inc(kv_high, 1)

            def mixing(r, n):
                wait(act, energy_done, r, upto(n + 1))
                wait(act, eo_done, r, upto_batches(n - 1))
                nc.scalar.activation(energy[:, :], e_ps[:, 0:P], ACT.Copy, scale=ATT_SCALE).then_inc(energy_ready, 1)

            def mixing_2(r, n):
                wait(act, eo_done, r, upto_batches(n + 1))
                wait(act, mix_done, r, upto_batches(n - 1))
                nc.scalar.activation(eo[:, :], e_ps[:, 0:EMB], ACT.Copy).then_inc(eo_ready, 1)

            def mixing_3(r, n):
                wait(act, mix_done, r, upto_batches(n + 1))
                wait(act, att_done, r, upto(n - 1))
                nc.scalar.activation(mix_h[:, :, :], kv_ps[:, :], ACT.Copy).then_inc(mix_high, 1)

            def xnT_high_half(r, n):
                wait(act, xn_turned, r, upto(n + 1))
                wait(act, att_done, r, upto(n - 1))
                for k in range(EC):
                    nc.scalar.activation(xnT_h[:, n % 2, k, :], work_ps[k][:, :], ACT.Copy).then_inc(xnT_high, 1)

            def x2T_high_half(r, n):
                wait(act, x2n_turned, r, upto(n + 1))
                wait(act, up_done, r, upto(n - 1, FC))
                for k in range(EC):
                    nc.scalar.activation(x2T_h[:, n % 2, k, :], work_ps[k][:, :], ACT.Copy).then_inc(x2T_high, 1)

            def step(r, i):
                for c in range(FC):
                    if there(r, i):
                        rectify(r, i, c)
                        if c:
                            high_half(r, i, c - 1)
                        square(r, i, c)
                    if there(r, i + 2) and closes_batch(i + 2):
                        if c == 0:
                            mixing(r, i + 2)
                        if c == 1:
                            mixing_2(r, i + 2)
                        if c == 2:
                            mixing_3(r, i + 2)
                    if c == 5 and there(r, i + 3):
                        xnT_high_half(r, i + 3)
                    if c == 6 and there(r, i + 1):
                        x2T_high_half(r, i + 1)
                if there(r, i):
                    high_half(r, i, FC - 1)
                if there(r, i + 3):
                    kv_high_half(r, i + 3)
                if isinstance(r, int) and i == -2:
                    feed_forward_weights()

            steps(act, step)

        @block.vector
        def _(dve):
            def as_f32(half):
                return half.bitcast(f32)

            nc.vector.memset(credit[:, 0:1], 0.0).then_inc(y_free, 2)
            for n, s in enumerate(x1_free):
                nc.vector.memset(credit[:, 1 + n:2 + n], 0.0).then_inc(s, 16)
            dve.wait_ge(wkv_high, 1)
            nc.vector.tensor_tensor(wkv_l[:, :, :], wkv_raw[:, :].rearrange("p (k n) -> p k n", k=EC),
                                    as_f32(wkv_h[:, :, :]), ALU.subtract).then_inc(wkv_ready, 1)

            def feed_forward_weights():
                dve.wait_ge(wff_high, 1)
                nc.vector.tensor_tensor(wup_l[:, :, :], wup_raw.rearrange("p (k n) -> p k n", k=EC),
                                        as_f32(wup_h[:, :, :]), ALU.subtract).then_inc(wff_ready, 1)
                dve.wait_ge(wff_high, 2)
                nc.vector.tensor_tensor(wdn_l[:, :, :], wdn_raw.rearrange("p (k n) -> p k n", k=FC),
                                        as_f32(wdn_h[:, :, :]), ALU.subtract).then_inc(wff_ready, 1)

            def kv_low_half(r, n):
                wait(dve, kv_high, r, upto(n + 1))
                src = kv_ps[:, :].rearrange("p (a d) -> p a d", d=HEAD)
                high = kv[:, :, :, 0, :].rearrange("p t s d -> p (t s) d")
                low = kv[:, :, :, 1, :].rearrange("p t s d -> p (t s) d")
                nc.vector.tensor_tensor(low, src, as_f32(high), ALU.subtract).then_inc(kv_ready, 1)

            def moments(r, n, which):
                wait(dve, (xn_ready, x2n_ready)[which], r, upto(n))
                for t in range(TILES):
                    last = nc.vector.bn_stats(stat[which][:, t, :], (xs, x1)[which][:, n % RING, t * EMB:(t + 1) * EMB])
                last.then_inc(stats_done[which], 1)
                wait(dve, stats_done[which], r, upto(n + 1))
                nc.vector.memset(credit[:, 1 + RING + which:2 + RING + which], 0.0)
                for t in range(TILES):
                    last = nc.vector.bn_aggr(mv[which][:, t, :], stat[which][:, t, :])
                last.then_inc(moments_ready[which], 1)

            def normalise(r, n, which):
                wait(dve, rstd_ready[which], r, upto(n + 1))
                wait(dve, (xn_turned, x2n_turned)[which], r, upto(n))
                for t in range(TILES):
                    cols = slice(t * EMB, (t + 1) * EMB)
                    last = nc.vector.tensor_scalar((xn, x2n)[which][:, cols], (xs, x1)[which][:, n % RING, cols],
                                                   mv[which][:, t, 0:1], rstd[which][:, t:t + 1],
                                                   ALU.subtract, ALU.mult)
                last.then_inc((xn_ready, x2n_ready)[which], 1)

            def residual(r, n):
                wait(dve, att_done, r, upto(n + 1))
                wait(dve, x1_free[n % RING], r, upto_slot(n))
                for k in range(2):
                    cols = slice(k * 512, (k + 1) * 512)
                    last = nc.vector.tensor_tensor(x1[:, n % RING, cols], work_ps[k][:, :], xs[:, n % RING, cols],
                                                   ALU.add)
                last.then_inc(x1_ready, 1)
                wait(dve, x1_ready, r, upto(n + 1))

            def xnT_low_half(r, n):
                for k in range(EC):
                    wait(dve, xnT_high, r, upto(n, EC, k + 1))
                    last = nc.vector.tensor_tensor(xnT_l[:, n % 2, k, :], work_ps[k][:, :],
                                                   as_f32(xnT_h[:, n % 2, k, :]), ALU.subtract)
                last.then_inc(xnT_ready, 1)

            def x2T_low_half(r, n):
                for k in range(EC):
                    wait(dve, x2T_high, r, upto(n, EC, k + 1))
                    last = nc.vector.tensor_tensor(x2T_l[:, n % 2, k, :], work_ps[k][:, :],
                                                   as_f32(x2T_h[:, n % 2, k, :]), ALU.subtract)
                last.then_inc(x2T_ready, 1)

            def mixing_low(r, n):
                wait(dve, mix_high, r, upto_batches(n + 1))
                nc.vector.tensor_tensor(mix_l[:, :, :], kv_ps[:, :].rearrange("p (k n) -> p k n", k=EC),
                                        as_f32(mix_h[:, :, :]), ALU.subtract).then_inc(mix_ready, 1)

            PAIR_OPS = 2 * (NUM_STEPS + 1)
            COUNTED = PAIR_OPS - 2

            def spikes(r, n, pair, ops):
                for o in ops:
                    level, a = o // 2, o % 2
                    y = y_ps[pair][:, a * EMB:(a + 1) * EMB]
                    acc = cnt[:, pair, a, :]
                    cols = slice((2 * pair + a) * EMB, (2 * pair + a + 1) * EMB)
                    if o == 0:
                        wait(dve, y_done, r, upto(n, 2, pair + 1))
                        if pair:
                            wait(dve, out_ready, r, upto(n, 2, 1))
                    if 2 <= o < PAIR_OPS - 1:
                        wait(dve, count_step, r, upto(n, 2 * COUNTED, pair * COUNTED + o - 1))
                    if o == PAIR_OPS - 1:
                        wait(dve, y_free, r, upto(n, 2, pair + 3))
                    if level == 0:
                        nc.vector.tensor_scalar(acc, y, THETA[0], None, ALU.is_gt).then_inc(count_step, 1)
                    elif level < NUM_STEPS:
                        nc.vector.scalar_tensor_tensor(acc, y, THETA[level], acc, ALU.is_gt, ALU.add)\
                            .then_inc(y_free if o == PAIR_OPS - 3 else count_step, 1)
                    else:
                        nc.vector.scalar_tensor_tensor(x1[:, n % RING, cols], acc, 1.0 / NUM_STEPS,
                                                       x1[:, n % RING, cols], ALU.mult, ALU.add)\
                            .then_inc(out_ready if o == PAIR_OPS - 1 else count_step, 1)

            def step(r, i):
                if there(r, i + 3):
                    slot = (i + 3) % RING
                    wait(dve, x_loaded[slot], r, upto_slot(i + 3))
                    moments(r, i + 3, 0)
                if there(r, i + 2) and closes_batch(i + 2):
                    mixing_low(r, i + 2)
                if there(r, i + 3):
                    normalise(r, i + 3, 0)
                if there(r, i + 1):
                    residual(r, i + 1)
                    moments(r, i + 1, 1)
                if there(r, i - 1):
                    spikes(r, i - 1, 0, range(0, PAIR_OPS // 2))
                if there(r, i + 1):
                    normalise(r, i + 1, 1)
                if there(r, i + 3):
                    xnT_low_half(r, i + 3)
                if there(r, i - 1):
                    spikes(r, i - 1, 0, range(PAIR_OPS // 2, PAIR_OPS))
                if there(r, i + 1):
                    x2T_low_half(r, i + 1)
                if there(r, i + 3):
                    kv_low_half(r, i + 3)
                if there(r, i - 1):
                    spikes(r, i - 1, 1, range(PAIR_OPS))
                if isinstance(r, int) and i == -2:
                    feed_forward_weights()

            steps(dve, step)

        @block.tensor
        def _(pe):
            mm = nc.tensor.matmul
            pe.wait_ge(ident_ready, 1)

            def three(dst, a, b, start, stop):
                mm(dst, a[0], b[0], start=start, stop=False)
                mm(dst, a[0], b[1], start=False, stop=False)
                return mm(dst, a[1], b[0], start=False, stop=stop)

            def turn_first(r, n):
                wait(pe, xn_ready, r, upto(n + 1))
                wait(pe, x1_ready, r, upto(n - 1))
                if not there(r, n - 2):
                    wait(pe, xnT_ready, r, upto(n))
                for k in range(EC):
                    for t in range(TILES):
                        at = t * EMB + k * P
                        last = nc.tensor.transpose(work_ps[k][:, t * P:(t + 1) * P], xn[:, at:at + P], ident[:, :])
                last.then_inc(xn_turned, 1)

            def turn_second(r, n):
                wait(pe, x2n_ready, r, upto(n + 1))
                if there(r, n + 2):
                    wait(pe, xnT_ready, r, upto(n + 3))
                for k in range(EC):
                    for t in range(TILES):
                        at = t * EMB + k * P
                        last = nc.tensor.transpose(work_ps[k][:, t * P:(t + 1) * P], x2n[:, at:at + P], ident[:, :])
                last.then_inc(x2n_turned, 1)

            def project_kv(r, n):
                wait(pe, xnT_ready, r, upto(n + 1))
                wait(pe, kv_ready, r, upto(n))
                wait(pe, mix_ready, r, upto_batches(n))
                if isinstance(r, int) and n == 0:
                    pe.wait_ge(wkv_ready, 1)
                for t in range(TILES):
                    cols = slice(t * P, (t + 1) * P)
                    for k in range(EC):
                        last = three(kv_ps[:, cols], (xnT_h[:, n % 2, k, cols], xnT_l[:, n % 2, k, cols]),
                                     (wkv_h[:, k, :], wkv_l[:, k, :]), k == 0, k == EC - 1)
                last.then_inc(kv_done, 1)

            def energy_sum(r, n):
                wait(pe, kv_ready, r, upto(n + 1))
                if not closes_batch(n):
                    wait(pe, eo_ready, r, upto_batches(n))
                for t in range(TILES):
                    flat = [kv[:, t, s, :, :].rearrange("p h d -> p (h d)") for s in range(2)]
                    last = mm(e_ps[:, 0:P], flat[1], flat[0], start=(t == 0 and not closes_batch(n)),
                              stop=(t == TILES - 1 and closes_batch(n)))
                last.then_inc(energy_done, 1)

            def energy_out(r, n):
                wait(pe, energy_ready, r, upto_batches(n + 1))
                if isinstance(r, int) and n == PER_BATCH - 1:
                    pe.wait_ge(w_loaded["o"], 16)
                mm(e_ps[:, 0:EMB], energy[:, :], wo2[:, :], start=True, stop=True).then_inc(eo_done, 1)

            def mixing_matrix(r, n):
                wait(pe, eo_ready, r, upto_batches(n + 1))
                if isinstance(r, int) and n == PER_BATCH - 1:
                    pe.wait_ge(w_loaded["q"], 16)
                for k in range(EC):
                    last = mm(kv_ps[:, k * EMB:(k + 1) * EMB], wq2[:, k * P:(k + 1) * P], eo[:, :],
                              start=True, stop=True)
                last.then_inc(mix_done, 1)

            def attend(r, n):
                wait(pe, mix_ready, r, upto_batches(n + PER_BATCH))
                wait(pe, x2T_ready, r, upto(n))
                if there(r, n + 1):
                    wait(pe, xnT_ready, r, upto(n + 2))
                for t in range(TILES):
                    cols = slice(t * P, (t + 1) * P)
                    for k in range(EC):
                        last = three(work_ps[t // 2][:, (t % 2) * EMB:(t % 2 + 1) * EMB],
                                     (xnT_h[:, n % 2, k, cols], xnT_l[:, n % 2, k, cols]),
                                     (mix_h[:, k, :], mix_l[:, k, :]), k == 0, k == EC - 1)
                last.then_inc(att_done, 1)

            def project_up(r, i, c):
                if c == 0:
                    wait(pe, x2T_ready, r, upto(i + 1))
                    if isinstance(r, int) and i == 0:
                        pe.wait_ge(wff_ready, 2)
                wait(pe, relu_done, r, upto(i, FC, c - 1))
                for k in range(EC):
                    cols = slice(c * P, (c + 1) * P)
                    last = three(hid_ps[c % 2][:, :], (wup_h[:, k, cols], wup_l[:, k, cols]),
                                 (x2T_h[:, i % 2, k, :], x2T_l[:, i % 2, k, :]), k == 0, k == EC - 1)
                last.then_inc(up_done, 1)

            def project_down(r, n, c):
                t, half = c // 2, c % 2
                if c < 2:
                    wait(pe, hid_ready, r, upto(n, FC, (c + 1) * FC // 2))
                if c % 4 == 0:
                    wait(pe, y_free, r, upto(n, 2, t // 2 + 1))
                dst = y_ps[t // 2][:, (t % 2) * EMB:(t % 2 + 1) * EMB]
                cols = slice(t * P, (t + 1) * P)
                for f in range(half * FC // 2, (half + 1) * FC // 2):
                    last = three(dst, (hid_h[:, n % 2, f, cols], hid_l[:, n % 2, f, cols]),
                                 (wdn_h[:, f, :], wdn_l[:, f, :]), f == 0, f == FC - 1)
                if c % 4 == 3:
                    last.then_inc(y_done, 1)

            def step(r, i):
                for c in range(FC):
                    if there(r, i):
                        project_up(r, i, c)
                    if there(r, i - 1):
                        project_down(r, i - 1, c)
                    if c == 0 and there(r, i + 2):
                        energy_sum(r, i + 2)
                    if there(r, i + 2) and closes_batch(i + 2):
                        if c == 1:
                            energy_out(r, i + 2)
                        if c == 2:
                            mixing_matrix(r, i + 2)
                    if c == 3 and there(r, i + 1):
                        attend(r, i + 1)
                    if c == 5 and there(r, i + 3):
                        turn_first(r, i + 3)
                    if c == 6 and there(r, i + 1):
                        turn_second(r, i + 1)
                    if c == 7 and there(r, i + 3):
                        project_kv(r, i + 3)

            steps(pe, step)


def kernel(L0_attn_x, L0_attn_wq, L0_attn_wk, L0_attn_wv, L0_attn_wo, L0_ffn_W_fc, L0_ffn_W_proj):
    import concourse.bacc as bacc
    from concourse.bass_utils import run_bass_kernel_spmd

    def chunks(w):
        rows, n = w.shape
        return np.ascontiguousarray(w.reshape(rows // P, P, n).transpose(1, 0, 2).reshape(P, -1))

    x, wq, wk, wv, wo, w_fc, w_proj = (np.asarray(a) for a in (
        L0_attn_x, L0_attn_wq, L0_attn_wk, L0_attn_wv, L0_attn_wo, L0_ffn_W_fc, L0_ffn_W_proj))
    arrays = {
        "x": np.ascontiguousarray(x.reshape(-1, EMB)),
        "w_kv": chunks(np.concatenate([wk.T, wv.T], axis=1)),
        "w_q": np.concatenate([wq, wq], axis=0),
        "w_o": np.concatenate([wo.T, wo.T], axis=0),
        "w_up": chunks(w_fc.T),
        "w_down": chunks(w_proj.T),
    }
    nc = bacc.Bacc("TRN2", target_bir_lowering=False, num_devices=1)
    args = [nc.dram_tensor(f"{n}_dram", a.shape, mybir.dt.float32, kind="ExternalInput").ap()
            for n, a in arrays.items()]
    out = nc.dram_tensor("out_dram", (BATCHES * SEQ, EMB), mybir.dt.float32, kind="ExternalOutput").ap()
    build(nc, *args, out)
    r = run_bass_kernel_spmd(nc, [{f"{n}_dram": a for n, a in arrays.items()}], core_ids=[0])
    return r.results[0]["out_dram"].reshape(BATCHES, SEQ, EMB)
```

```python
import concourse.bass as bass
from concourse import mybir
from contextlib import ExitStack
import math
import numpy as np


BATCHES, SEQ, EMB, HEAD, HID = 8, 1024, 256, 64, 1024
P = 128
GROUP = 512
TILES = GROUP // P
GROUPS = BATCHES * SEQ // GROUP
PER_BATCH = SEQ // GROUP
EC = EMB // P
FC = HID // P
GE = TILES * EMB
RING = 4
EPS = 1e-5
ATT_SCALE = math.sqrt(3.0 / HEAD)
BETA, THRESHOLD, NUM_STEPS = 0.9, 1.0, 5
UNROLL = 4
FIRST = 1
LOOPS = (GROUPS - 3 - FIRST) // UNROLL
LAST = FIRST + UNROLL * LOOPS


def spike_counts(y):
    y, one = np.float32(y), np.float32(1.0)
    mem, count = np.float32(0.0), 0
    for _ in range(NUM_STEPS):
        reset = one if mem > np.float32(THRESHOLD) else np.float32(0.0)
        mem = np.float32(np.float32(np.float32(BETA) * mem) + y) - reset * np.float32(THRESHOLD)
        count += int(mem > np.float32(THRESHOLD))
    return count


def spike_thresholds():
    found = []
    for n in range(1, NUM_STEPS + 1):
        low, high = (int(np.float32(v).view(np.int32)) for v in (0.01, 4.0))
        while high - low > 1:
            mid = (low + high) // 2
            if spike_counts(np.int32(mid).view(np.float32)) >= n:
                high = mid
            else:
                low = mid
        found.append(float(np.int32(low).view(np.float32)))
    return found


def build(nc, x, w_kv, w_qq, w_o, w_up, w_down, out):
    f32, f32r = mybir.dt.float32, mybir.dt.float32r
    ACT, ALU = mybir.ActivationFunctionType, mybir.AluOpType
    THETA = spike_thresholds()
    x_d = x.rearrange("(g p t) e -> g p (t e)", p=P, t=TILES)
    out_d = out.rearrange("(g p t) e -> g p (t e)", p=P, t=TILES)

    with ExitStack() as ctx:
        def sb(name, shape, dt=f32):
            return ctx.enter_context(nc.sbuf_tensor(name, shape, dt))

        def bank(name):
            return ctx.enter_context(nc.psum_tensor(name, [P, 512], f32))

        def sem(name):
            return ctx.enter_context(nc.semaphore(name))

        wkv_raw = sb("wkv_raw", [P, EC * 2 * HEAD])
        wqq_raw = sb("wqq_raw", [P, EC * 2 * HEAD])
        wo2 = sb("wo2", [P, EMB])
        wkv_h, wkv_l = (sb(f"wkv_{s}", [P, EC, 2 * HEAD], f32r) for s in "hl")
        wqq_h, wqq_l = (sb(f"wqq_{s}", [P, EC, 2 * HEAD], f32r) for s in "hl")
        wup_h, wup_l = (sb(f"wup_{s}", [P, EC, HID], f32r) for s in "hl")
        wdn_h, wdn_l = (sb(f"wdn_{s}", [P, FC, EMB], f32r) for s in "hl")
        ident = sb("ident", [P, P])
        xs = sb("xs", [P, RING, GE])
        x1 = sb("x1", [P, RING, GE])
        xn = sb("xn", [P, GE])
        x2n = sb("x2n", [P, GE])
        xnT_h, xnT_l = (sb(f"xnT_{s}", [P, 2, EC, GROUP], f32r) for s in "hl")
        x2T_h, x2T_l = (sb(f"x2T_{s}", [P, 2, EC, GROUP], f32r) for s in "hl")
        qT = sb("qT", [P, 2, GROUP], f32r)
        kvT = sb("kvT", [P, GROUP])
        kv = sb("kv", [P, TILES, 2, 2, HEAD], f32r)
        energy_half = sb("energy_half", [P, HEAD])
        energy = sb("energy", [P, 2, HEAD])
        eo_h, eo_l = (sb(f"eo_{s}", [P, EMB], f32r) for s in "hl")
        relu = sb("relu", [P, 2, GROUP])
        hid = sb("hid", [P, 4, GROUP])
        hid_h, hid_l = (sb(f"hid_{s}", [P, 2, FC, GROUP], f32r) for s in "hl")
        wup_raw = hid[:, :, :].rearrange("p s n -> p (s n)")
        wdn_raw = x1[:, 2:4, :].rearrange("p s n -> p (s n)")
        cnt = sb("cnt", [P, 2, 2, EMB])
        credit = sb("credit", [P, 1 + RING + 2])
        stat = [sb(f"stat{n}", [P, TILES, 6]) for n in (1, 2)]
        mv = [sb(f"mv{n}", [P, TILES, 2]) for n in (1, 2)]
        ve = [sb(f"ve{n}", [P, TILES]) for n in (1, 2)]
        rstd = [sb(f"rstd{n}", [P, TILES]) for n in (1, 2)]
        neg_half = sb("neg_half", [P, TILES])
        eps = sb("eps", [P, TILES])

        hid_ps = [bank(f"hid_ps{n}") for n in range(2)]
        y_ps = [bank(f"y_ps{n}") for n in range(2)]
        work_ps = [bank(f"work_ps{n}") for n in range(2)]
        kv_ps = bank("kv_ps")
        e_ps = bank("e_ps")

        def turn_banks(r, n):
            return {1: hid_ps, 2: hid_ps}.get(n, work_ps) if isinstance(r, int) else work_ps

        def turn2_banks(r, n):
            return {0: y_ps}.get(n, work_ps) if isinstance(r, int) else work_ps

        def kv_bank(r, n):
            return {1: y_ps[0]}.get(n, kv_ps) if isinstance(r, int) else kv_ps

        x_loaded = [sem(f"x_loaded{n}") for n in range(RING)]
        x1_free = [sem(f"x1_free{n}") for n in range(RING)]
        w_loaded = {n: sem(f"w_loaded_{n}") for n in ("kv", "qq", "o", "up", "down")}
        ident_zero, ident_ready, half_ready = sem("ident_zero"), sem("ident_ready"), sem("half_ready")
        wkv_high, wkv_ready = sem("wkv_high"), sem("wkv_ready")
        wqq_high, wqq_ready = sem("wqq_high"), sem("wqq_ready")
        wup_high, wup_ready = sem("wup_high"), sem("wup_ready")
        wdn_high, wdn_ready = sem("wdn_high"), sem("wdn_ready")
        stats_done = [sem(f"stats{n}_done") for n in (1, 2)]
        moments_ready = [sem(f"moments{n}_ready") for n in (1, 2)]
        ve_ready = [sem(f"ve{n}_ready") for n in (1, 2)]
        rstd_ready = [sem(f"rstd{n}_ready") for n in (1, 2)]
        norm_ready = [sem("xn_ready"), sem("x2n_ready")]
        norm_turned = [sem("xn_turned"), sem("x2n_turned")]
        xnT_high, xnT_ready = sem("xnT_high"), sem("xnT_ready")
        x2T_high, x2T_ready = sem("x2T_high"), sem("x2T_ready")
        kvT_done, kvT_ready = sem("kvT_done"), sem("kvT_ready")
        kv_turned, kv_high, kv_ready = sem("kv_turned"), sem("kv_high"), sem("kv_ready")
        q_done, q_high, q_ready = sem("q_done"), sem("q_high"), sem("q_ready")
        energy_done, energy_out, energy_ready = sem("energy_done"), sem("energy_out"), sem("energy_ready")
        eo_done, eo_high, eo_ready = sem("eo_done"), sem("eo_high"), sem("eo_ready")
        att_done, x1_ready = sem("att_done"), sem("x1_ready")
        up_done, relu_done, hid_done = sem("up_done"), sem("relu_done"), sem("hid_done")
        hid_high, hid_ready = sem("hid_high"), sem("hid_ready")
        y_done, count_step, out_ready = sem("y_done"), sem("count_step"), sem("out_ready")
        y_free = sem("y_free")

        def counted(r, first, per_round):
            assert first > 0 or isinstance(r, int), first
            return r * per_round + first

        def upto(r, n, per=1, plus=0):
            return counted(r, per * n + plus, per * UNROLL)

        def upto_batches(r, n):
            return counted(r, n // PER_BATCH, UNROLL // PER_BATCH)

        def upto_slot(r, n):
            return counted(r, 16 * (n // RING + 1), 16 * UNROLL // RING)

        def steps(eng, step):
            for i in range(0, FIRST):
                step(0, i)
            with eng.Fori(0, LOOPS) as r:
                for j in range(UNROLL):
                    step(r, FIRST + j)
            for i in range(LAST, GROUPS + 1):
                step(0, i)

        def there(r, n):
            return not isinstance(r, int) or 0 <= n < GROUPS

        def is_first(r, i):
            return isinstance(r, int) and i == 0

        def closes_batch(n):
            return n % PER_BATCH == PER_BATCH - 1

        block = ctx.enter_context(nc.Block())

        @block.sync
        def _(sp):
            def load(r, n):
                if there(r, n - RING):
                    sp.wait_ge(x1_ready, upto(r, n - RING + 1))
                sp.dma_start(xs[:, n % RING, :], x_d[r * UNROLL + n, :, :]).then_inc(x_loaded[n % RING], 16)

            def store(r, n):
                sp.wait_ge(out_ready, upto(r, n + 1, 2))
                sp.dma_start(out_d[r * UNROLL + n, :, :], x1[:, n % RING, :]).then_inc(x1_free[n % RING], 16)

            def store_pair(n, pair):
                sp.wait_ge(out_ready, 2 * n + pair + 1)
                cols = slice(pair * GE // 2, (pair + 1) * GE // 2)
                sp.dma_start(out_d[n, :, cols], x1[:, n % RING, cols]).then_inc(x1_free[n % RING], 16)

            def step(r, i):
                if there(r, i + RING + 1):
                    load(r, i + RING + 1)
                if there(r, i - 1):
                    store(r, i - 1)

            load(0, 0)
            sp.dma_start(wkv_raw[:, :], w_kv).then_inc(w_loaded["kv"], 16)
            sp.dma_start(wqq_raw[:, :], w_qq).then_inc(w_loaded["qq"], 16)
            load(0, 1)
            sp.dma_start(wo2[:, :], w_o).then_inc(w_loaded["o"], 16)
            load(0, 2)
            sp.dma_start(wup_raw, w_up).then_inc(w_loaded["up"], 16)
            sp.dma_start(wdn_raw, w_down).then_inc(w_loaded["down"], 16)
            load(0, 3)
            for i in range(-1, FIRST):
                step(0, i)
            loops = (GROUPS - RING - 1 - FIRST) // UNROLL
            with sp.Fori(0, loops) as r:
                for j in range(UNROLL):
                    step(r, FIRST + j)
            for i in range(FIRST + UNROLL * loops, GROUPS):
                step(0, i)
            store_pair(GROUPS - 1, 0)
            store_pair(GROUPS - 1, 1)
            for n, s in enumerate(x1_free):
                sp.wait_ge(s, 16 * (GROUPS // RING + 1 + (n == (GROUPS - 1) % RING)))

        @block.gpsimd
        def _(pool):
            nc.gpsimd.memset(ident[:, :], 0.0).then_inc(ident_zero, 1)
            nc.gpsimd.memset(neg_half[:, :], -0.5).then_inc(half_ready, 1)
            nc.gpsimd.memset(eps[:, :], EPS).then_inc(half_ready, 1)
            pool.wait_ge(ident_zero, 1)
            nc.gpsimd.affine_select(out=ident[:, :], in_=ident[:, :], compare_op=ALU.not_equal, fill=1.0, base=0,
                                    pattern=[[-1, P]], channel_multiplier=1).then_inc(ident_ready, 1)
            pool.wait_ge(half_ready, 2)

            def inverse_deviation(r, n, which):
                pool.wait_ge(moments_ready[which], upto(r, n + 1))
                if there(r, n - 1):
                    pool.wait_ge(norm_ready[which], upto(r, n))
                nc.gpsimd.tensor_tensor(ve[which][:, :], mv[which][:, :, 1], eps[:, :], ALU.add)\
                    .then_inc(ve_ready[which], 1)
                pool.wait_ge(ve_ready[which], upto(r, n + 1))
                nc.gpsimd.tensor_tensor(rstd[which][:, :], ve[which][:, :], neg_half[:, :], ALU.pow)\
                    .then_inc(rstd_ready[which], 1)

            def low_half(r, i, c):
                pool.wait_ge(hid_high, upto(r, i, FC, c + 1))
                nc.gpsimd.tensor_tensor(hid_l[:, i % 2, c, :], hid[:, c % 4, :], hid_h[:, i % 2, c, :].bitcast(f32),
                                        ALU.subtract).then_inc(hid_ready, 1)

            def step(r, i):
                for c in range(FC):
                    if c == 1 and there(r, i + 3) and not is_first(r, i):
                        inverse_deviation(r, i + 3, 0)
                    if c == 4 and there(r, i + 1):
                        inverse_deviation(r, i + 1, 1)
                    if there(r, i):
                        low_half(r, i, c)

            inverse_deviation(0, 0, 0)
            inverse_deviation(0, 1, 0)
            inverse_deviation(0, 2, 0)
            inverse_deviation(0, 0, 1)
            inverse_deviation(0, 3, 0)
            steps(pool, step)

        @block.scalar
        def _(act):
            def high_half_of_weights(loaded, raw, high, out_high):
                act.wait_ge(loaded, 16)
                nc.scalar.activation(high[:, :, :], raw, ACT.Copy).then_inc(out_high, 1)

            def rectify(r, i, c):
                act.wait_ge(up_done, upto(r, i, FC, c + 1))
                if there(r, i - 1) or c > 1:
                    act.wait_ge(hid_done, upto(r, i, FC, c - 1))
                nc.scalar.activation(relu[:, c % 2, :], hid_ps[c % 2][:, :], ACT.Relu).then_inc(relu_done, 1)

            def square(r, i, c):
                act.wait_ge(relu_done, upto(r, i, FC, c + 1))
                if there(r, i - 1) or c > 3:
                    act.wait_ge(hid_ready, upto(r, i, FC, c - 3))
                nc.scalar.activation(hid[:, c % 4, :], relu[:, c % 2, :], ACT.Square).then_inc(hid_done, 1)

            def high_half(r, i, c):
                act.wait_ge(hid_done, upto(r, i, FC, c + 1))
                nc.scalar.activation(hid_h[:, i % 2, c, :], hid[:, c % 4, :], ACT.Copy).then_inc(hid_high, 1)

            def kvT_out(r, n):
                act.wait_ge(kvT_done, upto(r, n + 1))
                if there(r, n - 1):
                    act.wait_ge(kv_turned, upto(r, n))
                nc.scalar.activation(kvT[:, :], kv_bank(r, n)[:, :], ACT.Copy).then_inc(kvT_ready, 1)

            def kv_high_half(r, n):
                act.wait_ge(kv_turned, upto(r, n + 1))
                if there(r, n - 1):
                    act.wait_ge(energy_done, upto(r, n))
                src = kv_bank(r, n)[:, :].rearrange("p (a d) -> p a d", d=HEAD)
                dst = kv[:, :, :, 0, :].rearrange("p t s d -> p (t s) d")
                nc.scalar.activation(dst, src, ACT.Copy).then_inc(kv_high, 1)

            def q_high_half(r, n):
                act.wait_ge(q_done, upto(r, n + 1))
                if there(r, n - 2):
                    act.wait_ge(att_done, upto(r, n - 1))
                nc.scalar.activation(qT[:, n % 2, :], work_ps[0][:, :], ACT.Copy).then_inc(q_high, 1)

            def energy_first_half(r, n):
                act.wait_ge(energy_done, upto(r, n + 1))
                if there(r, n - PER_BATCH):
                    act.wait_ge(energy_ready, upto_batches(r, n - 1))
                nc.scalar.activation(energy_half[:, :], e_ps[:, 0:HEAD], ACT.Copy, scale=ATT_SCALE)\
                    .then_inc(energy_out, 1)

            def eo_high_half(r, n):
                act.wait_ge(eo_done, upto_batches(r, n + 1))
                if there(r, n - 2):
                    act.wait_ge(att_done, upto(r, n - 1))
                nc.scalar.activation(eo_h[:, :], e_ps[:, 0:EMB], ACT.Copy).then_inc(eo_high, 1)

            def xnT_high_half(r, n):
                act.wait_ge(norm_turned[0], upto(r, n + 1))
                if there(r, n - 2):
                    act.wait_ge(q_done, upto(r, n - 1))
                    act.wait_ge(kvT_done, upto(r, n - 1))
                for k in range(EC):
                    nc.scalar.activation(xnT_h[:, n % 2, k, :], turn_banks(r, n)[k][:, :], ACT.Copy).then_inc(xnT_high, 1)

            def x2T_high_half(r, n):
                act.wait_ge(norm_turned[1], upto(r, n + 1))
                if there(r, n - 2):
                    act.wait_ge(up_done, upto(r, n - 1, FC))
                for k in range(EC):
                    nc.scalar.activation(x2T_h[:, n % 2, k, :], turn2_banks(r, n)[k][:, :], ACT.Copy).then_inc(x2T_high, 1)

            def step(r, i):
                for c in range(FC):
                    if there(r, i):
                        rectify(r, i, c)
                        if c:
                            high_half(r, i, c - 1)
                        square(r, i, c)
                    if c == 0 and there(r, i + 2) and not is_first(r, i):
                        q_high_half(r, i + 2)
                    if there(r, i + 2) and closes_batch(i + 2):
                        if c == 1:
                            energy_first_half(r, i + 2)
                        if c == 2:
                            eo_high_half(r, i + 2)
                    if c == 4 and there(r, i + 3):
                        xnT_high_half(r, i + 3)
                    if c == 6 and there(r, i + 3):
                        kvT_out(r, i + 3)
                    if c == 6 and there(r, i + 1):
                        x2T_high_half(r, i + 1)
                if there(r, i):
                    high_half(r, i, FC - 1)
                if there(r, i + 3):
                    kv_high_half(r, i + 3)

            high_half_of_weights(w_loaded["kv"], wkv_raw[:, :], wkv_h, wkv_high)
            high_half_of_weights(w_loaded["qq"], wqq_raw[:, :], wqq_h, wqq_high)
            xnT_high_half(0, 0)
            high_half_of_weights(w_loaded["up"], wup_raw, wup_h, wup_high)
            kvT_out(0, 0)
            xnT_high_half(0, 1)
            q_high_half(0, 0)
            kv_high_half(0, 0)
            kvT_out(0, 1)
            q_high_half(0, 1)
            kv_high_half(0, 1)
            energy_first_half(0, PER_BATCH - 1)
            eo_high_half(0, PER_BATCH - 1)
            xnT_high_half(0, 2)
            high_half_of_weights(w_loaded["down"], wdn_raw, wdn_h, wdn_high)
            kvT_out(0, 2)
            q_high_half(0, 2)
            x2T_high_half(0, 0)
            kv_high_half(0, 2)
            steps(act, step)

        @block.vector
        def _(dve):
            def as_f32(half):
                return half.bitcast(f32)

            nc.vector.memset(credit[:, 0:1], 0.0).then_inc(y_free, 2)
            for n, s in enumerate(x1_free):
                nc.vector.memset(credit[:, 1 + n:2 + n], 0.0).then_inc(s, 16)
            def low_half_of_weights(out_high, raw, high, low, ready):
                dve.wait_ge(out_high, 1)
                nc.vector.tensor_tensor(low[:, :, :], raw.rearrange("p (k n) -> p k n", k=low.shape[1]),
                                        as_f32(high[:, :, :]), ALU.subtract).then_inc(ready, 1)

            def kv_low_half(r, n):
                dve.wait_ge(kv_high, upto(r, n + 1))
                src = kv_bank(r, n)[:, :].rearrange("p (a d) -> p a d", d=HEAD)
                high = kv[:, :, :, 0, :].rearrange("p t s d -> p (t s) d")
                low = kv[:, :, :, 1, :].rearrange("p t s d -> p (t s) d")
                nc.vector.tensor_tensor(low, src, as_f32(high), ALU.subtract).then_inc(kv_ready, 1)

            def moments(r, n, which):
                if there(r, n - 1):
                    dve.wait_ge(norm_ready[which], upto(r, n))
                for t in range(TILES):
                    last = nc.vector.bn_stats(stat[which][:, t, :], (xs, x1)[which][:, n % RING, t * EMB:(t + 1) * EMB])
                last.then_inc(stats_done[which], 1)
                dve.wait_ge(stats_done[which], upto(r, n + 1))
                nc.vector.memset(credit[:, 1 + RING + which:2 + RING + which], 0.0)
                for t in range(TILES):
                    last = nc.vector.bn_aggr(mv[which][:, t, :], stat[which][:, t, :])
                last.then_inc(moments_ready[which], 1)

            def normalise(r, n, which):
                dve.wait_ge(rstd_ready[which], upto(r, n + 1))
                if there(r, n - 1):
                    dve.wait_ge(norm_turned[which], upto(r, n))
                for t in range(TILES):
                    cols = slice(t * EMB, (t + 1) * EMB)
                    last = nc.vector.tensor_scalar((xn, x2n)[which][:, cols], (xs, x1)[which][:, n % RING, cols],
                                                   mv[which][:, t, 0:1], rstd[which][:, t:t + 1],
                                                   ALU.subtract, ALU.mult)
                last.then_inc(norm_ready[which], 1)

            def residual(r, n):
                dve.wait_ge(att_done, upto(r, n + 1))
                dve.wait_ge(x1_free[n % RING], upto_slot(r, n))
                for k in range(2):
                    cols = slice(k * 512, (k + 1) * 512)
                    last = nc.vector.tensor_tensor(x1[:, n % RING, cols], work_ps[k][:, :], xs[:, n % RING, cols],
                                                   ALU.add)
                last.then_inc(x1_ready, 1)
                dve.wait_ge(x1_ready, upto(r, n + 1))

            def xnT_low_half(r, n):
                for k in range(EC):
                    dve.wait_ge(xnT_high, upto(r, n, EC, k + 1))
                    last = nc.vector.tensor_tensor(xnT_l[:, n % 2, k, :], turn_banks(r, n)[k][:, :],
                                                   as_f32(xnT_h[:, n % 2, k, :]), ALU.subtract)
                last.then_inc(xnT_ready, 1)

            def x2T_low_half(r, n):
                for k in range(EC):
                    dve.wait_ge(x2T_high, upto(r, n, EC, k + 1))
                    last = nc.vector.tensor_tensor(x2T_l[:, n % 2, k, :], turn2_banks(r, n)[k][:, :],
                                                   as_f32(x2T_h[:, n % 2, k, :]), ALU.subtract)
                last.then_inc(x2T_ready, 1)

            def q_low_half(r, n):
                dve.wait_ge(q_high, upto(r, n + 1))
                nc.vector.tensor_tensor(qT[HEAD:P, n % 2, :], work_ps[0][HEAD:P, :],
                                        as_f32(qT[HEAD:P, n % 2, :]), ALU.subtract).then_inc(q_ready, 1)

            def energy_sum(r, n):
                dve.wait_ge(energy_out, upto_batches(r, n + 1))
                if there(r, n - PER_BATCH):
                    dve.wait_ge(eo_done, upto_batches(r, n - 1))
                for twice in range(2):
                    last = nc.vector.scalar_tensor_tensor(energy[:, twice, :], e_ps[:, HEAD:P], ATT_SCALE,
                                                          energy_half[:, :], ALU.mult, ALU.add)
                last.then_inc(energy_ready, 1)

            def eo_low_half(r, n):
                dve.wait_ge(eo_high, upto_batches(r, n + 1))
                nc.vector.tensor_tensor(eo_l[:, :], e_ps[:, 0:EMB], as_f32(eo_h[:, :]), ALU.subtract)\
                    .then_inc(eo_ready, 1)

            PAIR_OPS = 2 * (NUM_STEPS + 1)
            COUNTED = PAIR_OPS - 2

            def spikes(r, n, pair, ops):
                for o in ops:
                    level, a = o // 2, o % 2
                    y = y_ps[pair][:, a * EMB:(a + 1) * EMB]
                    acc = cnt[:, pair, a, :]
                    cols = slice((2 * pair + a) * EMB, (2 * pair + a + 1) * EMB)
                    if o == 0:
                        dve.wait_ge(y_done, upto(r, n, 2, pair + 1))
                        if pair:
                            dve.wait_ge(out_ready, upto(r, n, 2, 1))
                    if 2 <= o < PAIR_OPS - 1:
                        dve.wait_ge(count_step, upto(r, n, 2 * COUNTED, pair * COUNTED + o - 1))
                    if o == PAIR_OPS - 1:
                        dve.wait_ge(y_free, upto(r, n, 2, pair + 3))
                    if level == 0:
                        nc.vector.tensor_scalar(acc, y, THETA[0], None, ALU.is_gt).then_inc(count_step, 1)
                    elif level < NUM_STEPS:
                        nc.vector.scalar_tensor_tensor(acc, y, THETA[level], acc, ALU.is_gt, ALU.add)\
                            .then_inc(y_free if o == PAIR_OPS - 3 else count_step, 1)
                    else:
                        nc.vector.scalar_tensor_tensor(x1[:, n % RING, cols], acc, 1.0 / NUM_STEPS,
                                                       x1[:, n % RING, cols], ALU.mult, ALU.add)\
                            .then_inc(out_ready if o == PAIR_OPS - 1 else count_step, 1)

            def first_moments(r, n):
                dve.wait_ge(x_loaded[n % RING], upto_slot(r, n))
                moments(r, n, 0)

            def step(r, i):
                if there(r, i + 3) and not is_first(r, i):
                    first_moments(r, i + 3)
                if there(r, i + 2) and not is_first(r, i):
                    q_low_half(r, i + 2)
                if there(r, i + 2) and closes_batch(i + 2):
                    energy_sum(r, i + 2)
                if there(r, i + 3) and not is_first(r, i):
                    normalise(r, i + 3, 0)
                if there(r, i + 2) and closes_batch(i + 2):
                    eo_low_half(r, i + 2)
                if there(r, i + 1):
                    residual(r, i + 1)
                    moments(r, i + 1, 1)
                if there(r, i + 3):
                    xnT_low_half(r, i + 3)
                if there(r, i - 1):
                    spikes(r, i - 1, 0, range(0, PAIR_OPS // 2))
                if there(r, i + 1):
                    normalise(r, i + 1, 1)
                if there(r, i - 1):
                    spikes(r, i - 1, 0, range(PAIR_OPS // 2, PAIR_OPS))
                if there(r, i + 1):
                    x2T_low_half(r, i + 1)
                if there(r, i + 3):
                    kv_low_half(r, i + 3)
                if there(r, i - 1):
                    spikes(r, i - 1, 1, range(PAIR_OPS))

            first_moments(0, 0)
            low_half_of_weights(wkv_high, wkv_raw[:, :], wkv_h, wkv_l, wkv_ready)
            normalise(0, 0, 0)
            low_half_of_weights(wqq_high, wqq_raw[:, :], wqq_h, wqq_l, wqq_ready)
            first_moments(0, 1)
            xnT_low_half(0, 0)
            normalise(0, 1, 0)
            low_half_of_weights(wup_high, wup_raw, wup_h, wup_l, wup_ready)
            xnT_low_half(0, 1)
            q_low_half(0, 0)
            kv_low_half(0, 0)
            first_moments(0, 2)
            q_low_half(0, 1)
            kv_low_half(0, 1)
            normalise(0, 2, 0)
            energy_sum(0, PER_BATCH - 1)
            eo_low_half(0, PER_BATCH - 1)
            xnT_low_half(0, 2)
            residual(0, 0)
            moments(0, 0, 1)
            first_moments(0, 3)
            normalise(0, 0, 1)
            q_low_half(0, 2)
            x2T_low_half(0, 0)
            normalise(0, 3, 0)
            kv_low_half(0, 2)
            low_half_of_weights(wdn_high, wdn_raw, wdn_h, wdn_l, wdn_ready)
            steps(dve, step)

        @block.tensor
        def _(pe):
            mm = nc.tensor.matmul
            pe.wait_ge(ident_ready, 1)

            def three(dst, a, b, start, stop):
                mm(dst, a[0], b[0], start=start, stop=False)
                mm(dst, a[0], b[1], start=False, stop=False)
                return mm(dst, a[1], b[0], start=False, stop=stop)

            def turn_first(r, n):
                pe.wait_ge(norm_ready[0], upto(r, n + 1))
                if isinstance(r, int) and n == 2:
                    pe.wait_ge(xnT_ready, 2)
                if n >= 3 or not isinstance(r, int):
                    pe.wait_ge(x1_ready, upto(r, n - 1))
                for k in range(EC):
                    for t in range(TILES):
                        at = t * EMB + k * P
                        last = nc.tensor.transpose(turn_banks(r, n)[k][:, t * P:(t + 1) * P], xn[:, at:at + P],
                                                   ident[:, :])
                last.then_inc(norm_turned[0], 1)

            def turn_second(r, n):
                pe.wait_ge(norm_ready[1], upto(r, n + 1))
                if there(r, n + 2) and turn2_banks(r, n) is work_ps:
                    pe.wait_ge(xnT_ready, upto(r, n + 3))
                for k in range(EC):
                    for t in range(TILES):
                        at = t * EMB + k * P
                        last = nc.tensor.transpose(turn2_banks(r, n)[k][:, t * P:(t + 1) * P], x2n[:, at:at + P],
                                                   ident[:, :])
                last.then_inc(norm_turned[1], 1)

            def project_kv(r, n):
                pe.wait_ge(xnT_ready, upto(r, n + 1))
                if there(r, n - 2):
                    pe.wait_ge(kv_ready, upto(r, n))
                if isinstance(r, int) and n == 0:
                    pe.wait_ge(wkv_ready, 1)
                for k in range(EC):
                    last = three(kv_bank(r, n)[:, :], (wkv_h[:, k, :], wkv_l[:, k, :]),
                                 (xnT_h[:, n % 2, k, :], xnT_l[:, n % 2, k, :]), k == 0, k == EC - 1)
                last.then_inc(kvT_done, 1)

            def turn_kv(r, n):
                pe.wait_ge(kvT_ready, upto(r, n + 1))
                for t in range(TILES):
                    cols = slice(t * P, (t + 1) * P)
                    last = nc.tensor.transpose(kv_bank(r, n)[:, cols], kvT[:, cols], ident[:, :])
                last.then_inc(kv_turned, 1)

            def project_q(r, n):
                if isinstance(r, int) and n < 3:
                    pe.wait_ge(xnT_ready, n + 1)
                    pe.wait_ge(wqq_ready, 1)
                    if n == 1:
                        pe.wait_ge(q_ready, 1)
                    if n == 2:
                        pe.wait_ge(x1_ready, 1)
                else:
                    pe.wait_ge(x2T_ready, upto(r, n - 1))
                for k in range(EC):
                    last = three(work_ps[0][:, :], (wqq_h[:, k, :], wqq_l[:, k, :]),
                                 (xnT_h[:, n % 2, k, :], xnT_l[:, n % 2, k, :]), k == 0, k == EC - 1)
                last.then_inc(q_done, 1)

            def energy_sum(r, n):
                pe.wait_ge(kv_ready, upto(r, n + 1))
                if not closes_batch(n):
                    if there(r, n - PER_BATCH):
                        pe.wait_ge(eo_ready, upto_batches(r, n))
                for t in range(TILES):
                    flat = [kv[:, t, s, :, :].rearrange("p h d -> p (h d)") for s in range(2)]
                    last = mm(e_ps[:, 0:P], flat[1], flat[0], start=(t == 0 and not closes_batch(n)),
                              stop=(t == TILES - 1 and closes_batch(n)))
                last.then_inc(energy_done, 1)

            def energy_times_wo(r, n):
                pe.wait_ge(energy_ready, upto_batches(r, n + 1))
                if isinstance(r, int) and n == PER_BATCH - 1:
                    pe.wait_ge(w_loaded["o"], 16)
                mm(e_ps[:, 0:EMB], energy[:, :, :].rearrange("p t d -> p (t d)"), wo2[:, :],
                   start=True, stop=True).then_inc(eo_done, 1)

            def attend(r, n):
                pe.wait_ge(eo_ready, upto_batches(r, n + PER_BATCH))
                pe.wait_ge(q_ready, upto(r, n + 2 if there(r, n + 1) else n + 1))
                for t in range(TILES):
                    dst = work_ps[t // 2][:, (t % 2) * EMB:(t % 2 + 1) * EMB]
                    q = qT[:, n % 2, t * P:(t + 1) * P]
                    mm(dst, q, eo_h[:, :], start=True, stop=False)
                    last = mm(dst, q, eo_l[:, :], start=False, stop=True)
                last.then_inc(att_done, 1)

            def project_up(r, i, c):
                if c == 0:
                    pe.wait_ge(x2T_ready, upto(r, i + 1))
                    if isinstance(r, int) and i == 0:
                        pe.wait_ge(wup_ready, 1)
                if there(r, i - 1) or c > 1:
                    pe.wait_ge(relu_done, upto(r, i, FC, c - 1))
                for k in range(EC):
                    cols = slice(c * P, (c + 1) * P)
                    last = three(hid_ps[c % 2][:, :], (wup_h[:, k, cols], wup_l[:, k, cols]),
                                 (x2T_h[:, i % 2, k, :], x2T_l[:, i % 2, k, :]), k == 0, k == EC - 1)
                last.then_inc(up_done, 1)

            def project_down(r, n, c):
                t, half = c // 2, c % 2
                if isinstance(r, int) and n == 0 and c == 0:
                    pe.wait_ge(wdn_ready, 1)
                if c < 2:
                    pe.wait_ge(hid_ready, upto(r, n, FC, (c + 1) * FC // 2))
                if c % 4 == 0:
                    pe.wait_ge(y_free, upto(r, n, 2, t // 2 + 1))
                dst = y_ps[t // 2][:, (t % 2) * EMB:(t % 2 + 1) * EMB]
                cols = slice(t * P, (t + 1) * P)
                for f in range(half * FC // 2, (half + 1) * FC // 2):
                    last = three(dst, (hid_h[:, n % 2, f, cols], hid_l[:, n % 2, f, cols]),
                                 (wdn_h[:, f, :], wdn_l[:, f, :]), f == 0, f == FC - 1)
                if c % 4 == 3:
                    last.then_inc(y_done, 1)

            def step(r, i):
                for c in range(FC):
                    if there(r, i):
                        project_up(r, i, c)
                    if there(r, i - 1):
                        project_down(r, i - 1, c)
                    if c == 0 and there(r, i + 2) and not is_first(r, i):
                        project_q(r, i + 2)
                    if c == 1 and there(r, i + 2):
                        energy_sum(r, i + 2)
                    if c == 2 and there(r, i + 2) and closes_batch(i + 2):
                        energy_times_wo(r, i + 2)
                    if c == 3 and there(r, i + 1):
                        attend(r, i + 1)
                    if c == 4 and there(r, i + 3):
                        turn_first(r, i + 3)
                    if c == 6 and there(r, i + 3):
                        project_kv(r, i + 3)
                    if c == 6 and there(r, i + 1):
                        turn_second(r, i + 1)
                    if c == 7 and there(r, i + 3):
                        turn_kv(r, i + 3)

            turn_first(0, 0)
            project_kv(0, 0)
            turn_first(0, 1)
            project_q(0, 0)
            turn_kv(0, 0)
            project_kv(0, 1)
            project_q(0, 1)
            energy_sum(0, 0)
            turn_kv(0, 1)
            energy_sum(0, 1)
            energy_times_wo(0, PER_BATCH - 1)
            turn_first(0, 2)
            attend(0, 0)
            project_kv(0, 2)
            project_q(0, 2)
            turn_second(0, 0)
            turn_kv(0, 2)
            steps(pe, step)


def kernel(L0_attn_x, L0_attn_wq, L0_attn_wk, L0_attn_wv, L0_attn_wo, L0_ffn_W_fc, L0_ffn_W_proj):
    import concourse.bacc as bacc
    from concourse.bass_utils import run_bass_kernel_spmd

    def chunks(w):
        rows, n = w.shape
        return np.ascontiguousarray(w.reshape(rows // P, P, n).transpose(1, 0, 2).reshape(P, -1))

    x, wq, wk, wv, wo, w_fc, w_proj = (np.asarray(a) for a in (
        L0_attn_x, L0_attn_wq, L0_attn_wk, L0_attn_wv, L0_attn_wo, L0_ffn_W_fc, L0_ffn_W_proj))
    arrays = {
        "x": np.ascontiguousarray(x.reshape(-1, EMB)),
        "w_kv": chunks(np.concatenate([wk.T, wv.T], axis=1)),
        "w_qq": chunks(np.concatenate([wq.T, wq.T], axis=1)),
        "w_o": np.concatenate([wo.T, wo.T], axis=0),
        "w_up": chunks(w_fc.T),
        "w_down": chunks(w_proj.T),
    }
    nc = bacc.Bacc("TRN2", target_bir_lowering=False, num_devices=1)
    args = [nc.dram_tensor(f"{n}_dram", a.shape, mybir.dt.float32, kind="ExternalInput").ap()
            for n, a in arrays.items()]
    out = nc.dram_tensor("out_dram", (BATCHES * SEQ, EMB), mybir.dt.float32, kind="ExternalOutput").ap()
    build(nc, *args, out)
    r = run_bass_kernel_spmd(nc, [{f"{n}_dram": a for n, a in arrays.items()}], core_ids=[0])
    return r.results[0]["out_dram"].reshape(BATCHES, SEQ, EMB)
```

```python
import concourse.bass as bass
from concourse import mybir
from contextlib import ExitStack
import math
import numpy as np


BATCHES, SEQ, EMB, HEAD, HID = 8, 1024, 256, 64, 1024
P = 128
GROUP = 512
TILES = GROUP // P
GROUPS = BATCHES * SEQ // GROUP
PER_BATCH = SEQ // GROUP
EC = EMB // P
FC = HID // P
GE = TILES * EMB
RING = 4
EPS = 1e-5
ATT_SCALE = math.sqrt(3.0 / HEAD)
BETA, THRESHOLD, NUM_STEPS = 0.9, 1.0, 5
UNROLL = 4
FIRST = 1
LOOPS = (GROUPS - 3 - FIRST) // UNROLL
LAST = FIRST + UNROLL * LOOPS


def spike_counts(y):
    y, one = np.float32(y), np.float32(1.0)
    mem, count = np.float32(0.0), 0
    for _ in range(NUM_STEPS):
        reset = one if mem > np.float32(THRESHOLD) else np.float32(0.0)
        mem = np.float32(np.float32(np.float32(BETA) * mem) + y) - reset * np.float32(THRESHOLD)
        count += int(mem > np.float32(THRESHOLD))
    return count


def spike_thresholds():
    found = []
    for n in range(1, NUM_STEPS + 1):
        low, high = (int(np.float32(v).view(np.int32)) for v in (0.01, 4.0))
        while high - low > 1:
            mid = (low + high) // 2
            if spike_counts(np.int32(mid).view(np.float32)) >= n:
                high = mid
            else:
                low = mid
        found.append(float(np.int32(low).view(np.float32)))
    return found


def build(nc, x, w_kv, w_qq, w_o, w_up, w_down, out):
    f32, f32r = mybir.dt.float32, mybir.dt.float32r
    ACT, ALU = mybir.ActivationFunctionType, mybir.AluOpType
    THETA = spike_thresholds()
    x_d = x.rearrange("(g p t) e -> g p (t e)", p=P, t=TILES)
    out_d = out.rearrange("(g p t) e -> g p (t e)", p=P, t=TILES)

    with ExitStack() as ctx:
        def sb(name, shape, dt=f32):
            return ctx.enter_context(nc.sbuf_tensor(name, shape, dt))

        def bank(name):
            return ctx.enter_context(nc.psum_tensor(name, [P, 512], f32))

        def sem(name):
            return ctx.enter_context(nc.semaphore(name))

        wkv_raw = sb("wkv_raw", [P, EC * 2 * HEAD])
        wqq_raw = sb("wqq_raw", [P, EC * 2 * HEAD])
        wo2 = sb("wo2", [P, EMB])
        wkv_h, wkv_l = (sb(f"wkv_{s}", [P, EC, 2 * HEAD], f32r) for s in "hl")
        wqq_h, wqq_l = (sb(f"wqq_{s}", [P, EC, 2 * HEAD], f32r) for s in "hl")
        wup_h, wup_l = (sb(f"wup_{s}", [P, EC, HID], f32r) for s in "hl")
        wdn_h, wdn_l = (sb(f"wdn_{s}", [P, FC, EMB], f32r) for s in "hl")
        ident = sb("ident", [P, P])
        xs = sb("xs", [P, RING, GE])
        x1 = sb("x1", [P, RING, GE])
        xn = sb("xn", [P, GE])
        x2n = sb("x2n", [P, GE])
        xnT_h, xnT_l = (sb(f"xnT_{s}", [P, 2, EC, GROUP], f32r) for s in "hl")
        x2T_h, x2T_l = (sb(f"x2T_{s}", [P, 2, EC, GROUP], f32r) for s in "hl")
        qT = sb("qT", [P, 2, GROUP], f32r)
        kvT = sb("kvT", [P, GROUP])
        kv = sb("kv", [P, TILES, 2, 2, HEAD], f32r)
        energy_half = sb("energy_half", [P, HEAD])
        energy = sb("energy", [P, 2, HEAD])
        eo_h, eo_l = (sb(f"eo_{s}", [P, EMB], f32r) for s in "hl")
        relu = sb("relu", [P, 2, GROUP])
        hid = sb("hid", [P, 4, GROUP])
        hid_h, hid_l = (sb(f"hid_{s}", [P, 2, FC, GROUP], f32r) for s in "hl")
        wup_raw = hid[:, :, :].rearrange("p s n -> p (s n)")
        wdn_raw = x1[:, 2:4, :].rearrange("p s n -> p (s n)")
        cnt = sb("cnt", [P, 2, 2, EMB])
        credit = sb("credit", [P, 1 + RING + 2])
        stat = [sb(f"stat{n}", [P, TILES, 6]) for n in (1, 2)]
        mv = [sb(f"mv{n}", [P, TILES, 2]) for n in (1, 2)]
        ve = [sb(f"ve{n}", [P, TILES]) for n in (1, 2)]
        rstd = [sb(f"rstd{n}", [P, TILES]) for n in (1, 2)]
        neg_half = sb("neg_half", [P, TILES])

        hid_ps = [bank(f"hid_ps{n}") for n in range(2)]
        y_ps = [bank(f"y_ps{n}") for n in range(2)]
        work_ps = [bank(f"work_ps{n}") for n in range(2)]
        kv_ps = bank("kv_ps")
        e_ps = bank("e_ps")

        def turn_banks(r, n):
            return {1: hid_ps, 2: hid_ps}.get(n, work_ps) if isinstance(r, int) else work_ps

        def turn2_banks(r, n):
            return {0: y_ps}.get(n, work_ps) if isinstance(r, int) else work_ps

        def q_bank(r, n):
            return {0: work_ps[1]}.get(n, work_ps[0]) if isinstance(r, int) else work_ps[0]

        def kv_bank(r, n):
            return {1: y_ps[0]}.get(n, kv_ps) if isinstance(r, int) else kv_ps

        last_banks = work_ps + hid_ps

        first_pair_loaded = sem("first_pair_loaded")
        x_loaded = [sem(f"x_loaded{n}") for n in range(RING)]
        x1_free = [sem(f"x1_free{n}") for n in range(RING)]
        w_loaded = {n: sem(f"w_loaded_{n}") for n in ("kv", "qq", "o", "up", "down")}
        ident_zero, ident_ready, half_ready = sem("ident_zero"), sem("ident_ready"), sem("half_ready")
        wkv_high, wkv_ready = sem("wkv_high"), sem("wkv_ready")
        wqq_high, wqq_ready = sem("wqq_high"), sem("wqq_ready")
        wup_high, wup_ready = sem("wup_high"), sem("wup_ready")
        wdn_high, wdn_ready = sem("wdn_high"), sem("wdn_ready")
        stats_done = [sem(f"stats{n}_done") for n in (1, 2)]
        moments_ready = [sem(f"moments{n}_ready") for n in (1, 2)]
        aggregated = [sem(f"moments{n}_aggregated") for n in (1, 2)]
        rstd_ready = [sem(f"rstd{n}_ready") for n in (1, 2)]
        norm_ready = [sem("xn_ready"), sem("x2n_ready")]
        norm_turned = [sem("xn_turned"), sem("x2n_turned")]
        xnT_high, xnT_ready = sem("xnT_high"), sem("xnT_ready")
        x2T_high, x2T_ready = sem("x2T_high"), sem("x2T_ready")
        kvT_done, kvT_ready = sem("kvT_done"), sem("kvT_ready")
        kv_turned, kv_high, kv_ready = sem("kv_turned"), sem("kv_high"), sem("kv_ready")
        q_done, q_high, q_ready = sem("q_done"), sem("q_high"), sem("q_ready")
        energy_done, energy_out, energy_ready = sem("energy_done"), sem("energy_out"), sem("energy_ready")
        eo_done, eo_high, eo_ready = sem("eo_done"), sem("eo_high"), sem("eo_ready")
        att_done, x1_ready = sem("att_done"), sem("x1_ready")
        up_done, relu_done, hid_done = sem("up_done"), sem("relu_done"), sem("hid_done")
        hid_high, hid_ready = sem("hid_high"), sem("hid_ready")
        y_done, count_step, out_ready = sem("y_done"), sem("count_step"), sem("out_ready")
        last_y_done, last_step = sem("last_y_done"), sem("last_step")
        y_free = sem("y_free")

        def counted(r, first, per_round):
            assert first > 0 or isinstance(r, int), first
            return r * per_round + first

        def upto(r, n, per=1, plus=0):
            return counted(r, per * n + plus, per * UNROLL)

        def upto_batches(r, n):
            return counted(r, n // PER_BATCH, UNROLL // PER_BATCH)

        def upto_slot(r, n):
            return counted(r, 16 * (n // RING + 1), 16 * UNROLL // RING)

        def steps(eng, step):
            for i in range(0, FIRST):
                step(0, i)
            with eng.Fori(0, LOOPS) as r:
                for j in range(UNROLL):
                    step(r, FIRST + j)
            for i in range(LAST, GROUPS + 1):
                step(0, i)

        def there(r, n):
            return not isinstance(r, int) or 0 <= n < GROUPS

        def is_first(r, i):
            return isinstance(r, int) and i == 0

        def is_last(r, n):
            return isinstance(r, int) and n == GROUPS - 1

        def lane(r, n, which):
            return 1 if isinstance(r, int) and n == 1 else which

        def closes_batch(n):
            return n % PER_BATCH == PER_BATCH - 1

        block = ctx.enter_context(nc.Block())

        @block.sync
        def _(sp):
            def load(r, n):
                if there(r, n - RING):
                    sp.wait_ge(x1_ready, upto(r, n - RING + 1))
                sp.dma_start(xs[:, n % RING, :], x_d[r * UNROLL + n, :, :]).then_inc(x_loaded[n % RING], 16)

            def store(r, n):
                sp.wait_ge(out_ready, upto(r, n + 1, 2))
                sp.dma_start(out_d[r * UNROLL + n, :, :], x1[:, n % RING, :]).then_inc(x1_free[n % RING], 16)

            def store_last(first, end):
                sp.wait_ge(last_step, end * (NUM_STEPS + 1))
                n, cols = GROUPS - 1, slice(first * EMB, end * EMB)
                sp.dma_start(out_d[n, :, cols], x1[:, n % RING, cols]).then_inc(x1_free[n % RING], 16)

            def step(r, i):
                if there(r, i + RING + 1):
                    load(r, i + RING + 1)
                if there(r, i - 1):
                    store(r, i - 1)

            for pair, loaded in enumerate((first_pair_loaded, x_loaded[0])):
                cols = slice(pair * GE // 2, (pair + 1) * GE // 2)
                sp.dma_start(xs[:, 0, cols], x_d[0, :, cols]).then_inc(loaded, 16)
            sp.dma_start(wkv_raw[:, :], w_kv).then_inc(w_loaded["kv"], 16)
            load(0, 1)
            sp.dma_start(wqq_raw[:, :], w_qq).then_inc(w_loaded["qq"], 16)
            sp.dma_start(wo2[:, :], w_o).then_inc(w_loaded["o"], 16)
            load(0, 2)
            sp.dma_start(wup_raw, w_up).then_inc(w_loaded["up"], 16)
            sp.dma_start(wdn_raw, w_down).then_inc(w_loaded["down"], 16)
            load(0, 3)
            for i in range(-1, FIRST):
                step(0, i)
            loops = (GROUPS - RING - 1 - FIRST) // UNROLL
            with sp.Fori(0, loops) as r:
                for j in range(UNROLL):
                    step(r, FIRST + j)
            for i in range(FIRST + UNROLL * loops, GROUPS):
                step(0, i)
            store_last(0, 2)
            store_last(2, 3)
            store_last(3, 4)
            for n, s in enumerate(x1_free):
                sp.wait_ge(s, 16 * (GROUPS // RING + 1 + 2 * (n == (GROUPS - 1) % RING)))

        @block.gpsimd
        def _(pool):
            nc.gpsimd.memset(ident[:, :], 0.0).then_inc(ident_zero, 1)
            nc.gpsimd.memset(neg_half[:, :], -0.5).then_inc(half_ready, 1)
            pool.wait_ge(ident_zero, 1)
            nc.gpsimd.affine_select(out=ident[:, :], in_=ident[:, :], compare_op=ALU.not_equal, fill=1.0, base=0,
                                    pattern=[[-1, P]], channel_multiplier=1).then_inc(ident_ready, 1)
            pool.wait_ge(half_ready, 1)

            def inverse_deviation(r, n, which):
                pool.wait_ge(moments_ready[which], upto(r, n + 1))
                b = lane(r, n, which)
                nc.gpsimd.tensor_tensor(rstd[b][:, :], ve[b][:, :], neg_half[:, :], ALU.pow)\
                    .then_inc(rstd_ready[which], 1)

            def low_half_of_weights(out_high, raw, high, low, ready, h):
                pool.wait_ge(out_high, h + 1)
                chunks = slice(h * high.shape[1] // 2, (h + 1) * high.shape[1] // 2)
                nc.gpsimd.tensor_tensor(low[:, chunks, :], raw.rearrange("p (k n) -> p k n", k=low.shape[1])[:, chunks, :],
                                        high[:, chunks, :].bitcast(f32), ALU.subtract).then_inc(ready, 1)

            def low_half(r, i, c):
                pool.wait_ge(hid_high, upto(r, i, FC, c + 1))
                nc.gpsimd.tensor_tensor(hid_l[:, i % 2, c, :], hid[:, c % 4, :], hid_h[:, i % 2, c, :].bitcast(f32),
                                        ALU.subtract).then_inc(hid_ready, 1)

            def step(r, i):
                for c in range(FC):
                    if c == 1 and there(r, i + 3) and not is_first(r, i):
                        inverse_deviation(r, i + 3, 0)
                    if c == 4 and there(r, i + 1):
                        inverse_deviation(r, i + 1, 1)
                    if there(r, i):
                        low_half(r, i, c)

            inverse_deviation(0, 0, 0)
            inverse_deviation(0, 1, 0)
            inverse_deviation(0, 2, 0)
            low_half_of_weights(wup_high, wup_raw, wup_h, wup_l, wup_ready, 0)
            low_half_of_weights(wup_high, wup_raw, wup_h, wup_l, wup_ready, 1)
            low_half_of_weights(wdn_high, wdn_raw, wdn_h, wdn_l, wdn_ready, 0)
            inverse_deviation(0, 0, 1)
            low_half_of_weights(wdn_high, wdn_raw, wdn_h, wdn_l, wdn_ready, 1)
            inverse_deviation(0, 3, 0)
            steps(pool, step)

        @block.scalar
        def _(act):
            def high_half_of_weights(loaded, raw, high, out_high):
                act.wait_ge(loaded, 16)
                nc.scalar.activation(high[:, :, :], raw, ACT.Copy).then_inc(out_high, 1)

            def half_of_columns(loaded, raw, high, out_high, h):
                act.wait_ge(loaded, 16)
                chunks = slice(h * high.shape[1] // 2, (h + 1) * high.shape[1] // 2)
                nc.scalar.activation(high[:, chunks, :], raw.rearrange("p (k n) -> p k n", k=high.shape[1])[:, chunks, :],
                                     ACT.Copy).then_inc(out_high, 1)

            def rectify(r, i, c):
                act.wait_ge(up_done, upto(r, i, FC, c + 1))
                if there(r, i - 1) or c > 1:
                    act.wait_ge(hid_done, upto(r, i, FC, c - 1))
                nc.scalar.activation(relu[:, c % 2, :], hid_ps[c % 2][:, :], ACT.Relu).then_inc(relu_done, 1)

            def square(r, i, c):
                act.wait_ge(relu_done, upto(r, i, FC, c + 1))
                if there(r, i - 1) or c > 3:
                    act.wait_ge(hid_ready, upto(r, i, FC, c - 3))
                nc.scalar.activation(hid[:, c % 4, :], relu[:, c % 2, :], ACT.Square).then_inc(hid_done, 1)

            def high_half(r, i, c):
                act.wait_ge(hid_done, upto(r, i, FC, c + 1))
                nc.scalar.activation(hid_h[:, i % 2, c, :], hid[:, c % 4, :], ACT.Copy).then_inc(hid_high, 1)

            def kvT_out(r, n):
                act.wait_ge(kvT_done, upto(r, n + 1))
                if there(r, n - 1):
                    act.wait_ge(kv_turned, upto(r, n))
                nc.scalar.activation(kvT[:, :], kv_bank(r, n)[:, :], ACT.Copy).then_inc(kvT_ready, 1)

            def kv_high_half(r, n):
                act.wait_ge(kv_turned, upto(r, n + 1))
                if there(r, n - 1):
                    act.wait_ge(energy_done, upto(r, n))
                src = kv_bank(r, n)[:, :].rearrange("p (a d) -> p a d", d=HEAD)
                dst = kv[:, :, :, 0, :].rearrange("p t s d -> p (t s) d")
                nc.scalar.activation(dst, src, ACT.Copy).then_inc(kv_high, 1)

            def q_high_half(r, n):
                act.wait_ge(q_done, upto(r, n + 1))
                if there(r, n - 2):
                    act.wait_ge(att_done, upto(r, n - 1))
                nc.scalar.activation(qT[:, n % 2, :], q_bank(r, n)[:, :], ACT.Copy).then_inc(q_high, 1)

            def energy_first_half(r, n):
                act.wait_ge(energy_done, upto(r, n + 1))
                if there(r, n - PER_BATCH):
                    act.wait_ge(energy_ready, upto_batches(r, n - 1))
                nc.scalar.activation(energy_half[:, :], e_ps[:, 0:HEAD], ACT.Copy, scale=ATT_SCALE)\
                    .then_inc(energy_out, 1)

            def eo_high_half(r, n):
                act.wait_ge(eo_done, upto_batches(r, n + 1))
                if there(r, n - 2):
                    act.wait_ge(att_done, upto(r, n - 1))
                nc.scalar.activation(eo_h[:, :], e_ps[:, 0:EMB], ACT.Copy).then_inc(eo_high, 1)

            def xnT_high_half(r, n):
                act.wait_ge(norm_turned[0], upto(r, n + 1))
                if there(r, n - 2):
                    act.wait_ge(q_done, upto(r, n - 1))
                    act.wait_ge(kvT_done, upto(r, n - 1))
                for k in range(EC):
                    nc.scalar.activation(xnT_h[:, n % 2, k, :], turn_banks(r, n)[k][:, :], ACT.Copy).then_inc(xnT_high, 1)

            def x2T_high_half(r, n):
                act.wait_ge(norm_turned[1], upto(r, n + 1))
                if there(r, n - 2):
                    act.wait_ge(up_done, upto(r, n - 1, FC))
                for k in range(EC):
                    nc.scalar.activation(x2T_h[:, n % 2, k, :], turn2_banks(r, n)[k][:, :], ACT.Copy).then_inc(x2T_high, 1)

            def step(r, i):
                for c in range(FC):
                    if there(r, i):
                        rectify(r, i, c)
                        if c:
                            high_half(r, i, c - 1)
                        square(r, i, c)
                    if c == 0 and there(r, i + 2) and not is_first(r, i):
                        q_high_half(r, i + 2)
                    if there(r, i + 2) and closes_batch(i + 2):
                        if c == 1:
                            energy_first_half(r, i + 2)
                        if c == 2:
                            eo_high_half(r, i + 2)
                    if c == 4 and there(r, i + 3):
                        xnT_high_half(r, i + 3)
                    if c == 6 and there(r, i + 3):
                        kvT_out(r, i + 3)
                    if c == 6 and there(r, i + 1):
                        x2T_high_half(r, i + 1)
                if there(r, i):
                    high_half(r, i, FC - 1)
                if there(r, i + 3):
                    kv_high_half(r, i + 3)

            high_half_of_weights(w_loaded["kv"], wkv_raw[:, :], wkv_h, wkv_high)
            high_half_of_weights(w_loaded["qq"], wqq_raw[:, :], wqq_h, wqq_high)
            xnT_high_half(0, 0)
            xnT_high_half(0, 1)
            half_of_columns(w_loaded["up"], wup_raw, wup_h, wup_high, 0)
            kvT_out(0, 0)
            kv_high_half(0, 0)
            kvT_out(0, 1)
            q_high_half(0, 0)
            kv_high_half(0, 1)
            half_of_columns(w_loaded["up"], wup_raw, wup_h, wup_high, 1)
            energy_first_half(0, PER_BATCH - 1)
            q_high_half(0, 1)
            eo_high_half(0, PER_BATCH - 1)
            xnT_high_half(0, 2)
            half_of_columns(w_loaded["down"], wdn_raw, wdn_h, wdn_high, 0)
            kvT_out(0, 2)
            q_high_half(0, 2)
            kv_high_half(0, 2)
            half_of_columns(w_loaded["down"], wdn_raw, wdn_h, wdn_high, 1)
            x2T_high_half(0, 0)
            steps(act, step)

        @block.vector
        def _(dve):
            def as_f32(half):
                return half.bitcast(f32)

            nc.vector.memset(credit[:, 0:1], 0.0).then_inc(y_free, 2)
            for n, s in enumerate(x1_free):
                nc.vector.memset(credit[:, 1 + n:2 + n], 0.0).then_inc(s, 16)
            def low_half_of_weights(out_high, raw, high, low, ready):
                dve.wait_ge(out_high, 1)
                nc.vector.tensor_tensor(low[:, :, :], raw.rearrange("p (k n) -> p k n", k=low.shape[1]),
                                        as_f32(high[:, :, :]), ALU.subtract).then_inc(ready, 1)

            def kv_low_half(r, n):
                dve.wait_ge(kv_high, upto(r, n + 1))
                src = kv_bank(r, n)[:, :].rearrange("p (a d) -> p a d", d=HEAD)
                high = kv[:, :, :, 0, :].rearrange("p t s d -> p (t s) d")
                low = kv[:, :, :, 1, :].rearrange("p t s d -> p (t s) d")
                nc.vector.tensor_tensor(low, src, as_f32(high), ALU.subtract).then_inc(kv_ready, 1)

            def moments(r, n, which):
                b = lane(r, n, which)
                if there(r, n - 1) and b == which:
                    dve.wait_ge(norm_ready[which], upto(r, n, 2))
                if isinstance(r, int) and which == 1 and n == 0:
                    dve.wait_ge(norm_ready[0], 4)
                for t in range(TILES):
                    if t == TILES // 2 and isinstance(r, int) and n == 0 and which == 0:
                        dve.wait_ge(x_loaded[0], 16)
                    last = nc.vector.bn_stats(stat[b][:, t, :], (xs, x1)[which][:, n % RING, t * EMB:(t + 1) * EMB])
                last.then_inc(stats_done[which], 1)
                dve.wait_ge(stats_done[which], upto(r, n + 1))
                nc.vector.memset(credit[:, 1 + RING + which:2 + RING + which], 0.0)
                for t in range(TILES):
                    last = nc.vector.bn_aggr(mv[b][:, t, :], stat[b][:, t, :])
                last.then_inc(aggregated[which], 1)
                dve.wait_ge(aggregated[which], upto(r, n + 1))
                nc.vector.tensor_scalar(ve[b][:, :], mv[b][:, :, 1], EPS, None, ALU.add)\
                    .then_inc(moments_ready[which], 1)

            def normalise(r, n, which):
                b = lane(r, n, which)
                dve.wait_ge(rstd_ready[which], upto(r, n + 1))
                if there(r, n - 1) and b == which:
                    dve.wait_ge(norm_turned[which], upto(r, n))
                if isinstance(r, int) and which == 1 and n == 0:
                    dve.wait_ge(norm_turned[0], 2)
                for t in range(TILES):
                    cols = slice(t * EMB, (t + 1) * EMB)
                    last = nc.vector.tensor_scalar((xn, x2n)[b][:, cols], (xs, x1)[which][:, n % RING, cols],
                                                   mv[b][:, t, 0:1], rstd[b][:, t:t + 1],
                                                   ALU.subtract, ALU.mult)
                    if t % 2:
                        last.then_inc(norm_ready[which], 1)

            def residual(r, n):
                dve.wait_ge(att_done, upto(r, n + 1))
                dve.wait_ge(x1_free[n % RING], upto_slot(r, n))
                for k in range(2):
                    cols = slice(k * 512, (k + 1) * 512)
                    last = nc.vector.tensor_tensor(x1[:, n % RING, cols], work_ps[k][:, :], xs[:, n % RING, cols],
                                                   ALU.add)
                last.then_inc(x1_ready, 1)
                dve.wait_ge(x1_ready, upto(r, n + 1))

            def xnT_low_half(r, n):
                for k in range(EC):
                    dve.wait_ge(xnT_high, upto(r, n, EC, k + 1))
                    last = nc.vector.tensor_tensor(xnT_l[:, n % 2, k, :], turn_banks(r, n)[k][:, :],
                                                   as_f32(xnT_h[:, n % 2, k, :]), ALU.subtract)
                last.then_inc(xnT_ready, 1)

            def x2T_low_half(r, n):
                for k in range(EC):
                    dve.wait_ge(x2T_high, upto(r, n, EC, k + 1))
                    last = nc.vector.tensor_tensor(x2T_l[:, n % 2, k, :], turn2_banks(r, n)[k][:, :],
                                                   as_f32(x2T_h[:, n % 2, k, :]), ALU.subtract)
                last.then_inc(x2T_ready, 1)

            def q_low_half(r, n):
                dve.wait_ge(q_high, upto(r, n + 1))
                nc.vector.tensor_tensor(qT[HEAD:P, n % 2, :], q_bank(r, n)[HEAD:P, :],
                                        as_f32(qT[HEAD:P, n % 2, :]), ALU.subtract).then_inc(q_ready, 1)

            def energy_sum(r, n):
                dve.wait_ge(energy_out, upto_batches(r, n + 1))
                if there(r, n - PER_BATCH):
                    dve.wait_ge(eo_done, upto_batches(r, n - 1))
                for twice in range(2):
                    last = nc.vector.scalar_tensor_tensor(energy[:, twice, :], e_ps[:, HEAD:P], ATT_SCALE,
                                                          energy_half[:, :], ALU.mult, ALU.add)
                last.then_inc(energy_ready, 1)

            def eo_low_half(r, n):
                dve.wait_ge(eo_high, upto_batches(r, n + 1))
                nc.vector.tensor_tensor(eo_l[:, :], e_ps[:, 0:EMB], as_f32(eo_h[:, :]), ALU.subtract)\
                    .then_inc(eo_ready, 1)

            PAIR_OPS = 2 * (NUM_STEPS + 1)
            COUNTED = PAIR_OPS - 2

            def spikes(r, n, pair, ops):
                for o in ops:
                    level, a = o // 2, o % 2
                    y = y_ps[pair][:, a * EMB:(a + 1) * EMB]
                    acc = cnt[:, pair, a, :]
                    cols = slice((2 * pair + a) * EMB, (2 * pair + a + 1) * EMB)
                    if o == 0:
                        dve.wait_ge(y_done, upto(r, n, 2, pair + 1))
                        if pair:
                            dve.wait_ge(out_ready, upto(r, n, 2, 1))
                    if 2 <= o < PAIR_OPS - 1:
                        dve.wait_ge(count_step, upto(r, n, 2 * COUNTED, pair * COUNTED + o - 1))
                    if o == PAIR_OPS - 1:
                        dve.wait_ge(y_free, upto(r, n, 2, pair + 3))
                    if level == 0:
                        nc.vector.tensor_scalar(acc, y, THETA[0], None, ALU.is_gt).then_inc(count_step, 1)
                    elif level < NUM_STEPS:
                        nc.vector.scalar_tensor_tensor(acc, y, THETA[level], acc, ALU.is_gt, ALU.add)\
                            .then_inc(y_free if o == PAIR_OPS - 3 else count_step, 1)
                    else:
                        nc.vector.scalar_tensor_tensor(x1[:, n % RING, cols], acc, 1.0 / NUM_STEPS,
                                                       x1[:, n % RING, cols], ALU.mult, ALU.add)\
                            .then_inc(out_ready if o == PAIR_OPS - 1 else count_step, 1)

            def last_spikes(t):
                cols = slice(t * EMB, (t + 1) * EMB)
                acc, mine = cnt[:, t // 2, t % 2, :], x1[:, (GROUPS - 1) % RING, cols]
                y = last_banks[t][:, 0:EMB]
                dve.wait_ge(last_y_done, t + 1)
                dve.wait_ge(out_ready, 2 * (GROUPS - 1))
                nc.vector.tensor_scalar(acc, y, THETA[0], None, ALU.is_gt).then_inc(last_step, 1)
                for level in range(1, NUM_STEPS):
                    dve.wait_ge(last_step, t * (NUM_STEPS + 1) + level)
                    nc.vector.scalar_tensor_tensor(acc, y, THETA[level], acc, ALU.is_gt, ALU.add)\
                        .then_inc(last_step, 1)
                dve.wait_ge(last_step, t * (NUM_STEPS + 1) + NUM_STEPS)
                nc.vector.scalar_tensor_tensor(mine, acc, 1.0 / NUM_STEPS, mine, ALU.mult, ALU.add)\
                    .then_inc(last_step, 1)

            def first_moments(r, n):
                if isinstance(r, int) and n == 0:
                    dve.wait_ge(first_pair_loaded, 16)
                else:
                    dve.wait_ge(x_loaded[n % RING], upto_slot(r, n))
                moments(r, n, 0)

            def step(r, i):
                if there(r, i + 3) and not is_first(r, i):
                    first_moments(r, i + 3)
                if there(r, i + 2) and not is_first(r, i):
                    q_low_half(r, i + 2)
                if there(r, i + 2) and closes_batch(i + 2):
                    energy_sum(r, i + 2)
                if there(r, i + 3) and not is_first(r, i):
                    normalise(r, i + 3, 0)
                if there(r, i + 2) and closes_batch(i + 2):
                    eo_low_half(r, i + 2)
                if there(r, i + 1):
                    residual(r, i + 1)
                    moments(r, i + 1, 1)
                if there(r, i + 3):
                    xnT_low_half(r, i + 3)
                if is_last(r, i - 1):
                    for t in range(TILES):
                        last_spikes(t)
                    return
                if there(r, i - 1):
                    spikes(r, i - 1, 0, range(0, PAIR_OPS // 2))
                if there(r, i + 1):
                    normalise(r, i + 1, 1)
                if there(r, i - 1):
                    spikes(r, i - 1, 0, range(PAIR_OPS // 2, PAIR_OPS))
                if there(r, i + 1):
                    x2T_low_half(r, i + 1)
                if there(r, i + 3):
                    kv_low_half(r, i + 3)
                if there(r, i - 1):
                    spikes(r, i - 1, 1, range(PAIR_OPS))

            first_moments(0, 0)
            low_half_of_weights(wkv_high, wkv_raw[:, :], wkv_h, wkv_l, wkv_ready)
            first_moments(0, 1)
            normalise(0, 0, 0)
            normalise(0, 1, 0)
            xnT_low_half(0, 0)
            xnT_low_half(0, 1)
            low_half_of_weights(wqq_high, wqq_raw[:, :], wqq_h, wqq_l, wqq_ready)
            first_moments(0, 2)
            kv_low_half(0, 0)
            normalise(0, 2, 0)
            kv_low_half(0, 1)
            q_low_half(0, 0)
            energy_sum(0, PER_BATCH - 1)
            q_low_half(0, 1)
            eo_low_half(0, PER_BATCH - 1)
            xnT_low_half(0, 2)
            residual(0, 0)
            moments(0, 0, 1)
            q_low_half(0, 2)
            normalise(0, 0, 1)
            kv_low_half(0, 2)
            x2T_low_half(0, 0)
            first_moments(0, 3)
            normalise(0, 3, 0)
            steps(dve, step)

        @block.tensor
        def _(pe):
            mm = nc.tensor.matmul
            pe.wait_ge(ident_ready, 1)

            def three(dst, a, b, start, stop):
                mm(dst, a[0], b[0], start=start, stop=False)
                mm(dst, a[0], b[1], start=False, stop=False)
                return mm(dst, a[1], b[0], start=False, stop=stop)

            def keep_warm(rounds, idle=y_ps[1]):
                with pe.Fori(0, rounds) as _:
                    for _ in range(UNROLL):
                        nc.tensor.transpose(idle[:, 0:P], ident[:, :], ident[:, :])

            def turn_first(r, n):
                if isinstance(r, int) and n == 2:
                    pe.wait_ge(xnT_ready, 2)
                if n >= 3 or not isinstance(r, int):
                    pe.wait_ge(x1_ready, upto(r, n - 1))
                for t in range(TILES):
                    if t % 2 == 0:
                        pe.wait_ge(norm_ready[0], upto(r, n, 2, t // 2 + 1))
                    for k in range(EC):
                        at = t * EMB + k * P
                        last = nc.tensor.transpose(turn_banks(r, n)[k][:, t * P:(t + 1) * P],
                                                   (xn, x2n)[lane(r, n, 0)][:, at:at + P], ident[:, :])
                last.then_inc(norm_turned[0], 1)

            def turn_second(r, n):
                if there(r, n + 2) and turn2_banks(r, n) is work_ps:
                    pe.wait_ge(xnT_ready, upto(r, n + 3))
                for t in range(TILES):
                    if t % 2 == 0:
                        pe.wait_ge(norm_ready[1], upto(r, n, 2, t // 2 + 1))
                    for k in range(EC):
                        at = t * EMB + k * P
                        last = nc.tensor.transpose(turn2_banks(r, n)[k][:, t * P:(t + 1) * P], x2n[:, at:at + P],
                                                   ident[:, :])
                last.then_inc(norm_turned[1], 1)

            def project_kv(r, n):
                pe.wait_ge(xnT_ready, upto(r, n + 1))
                if there(r, n - 2):
                    pe.wait_ge(kv_ready, upto(r, n))
                if isinstance(r, int) and n == 0:
                    pe.wait_ge(wkv_ready, 1)
                for k in range(EC):
                    last = three(kv_bank(r, n)[:, :], (wkv_h[:, k, :], wkv_l[:, k, :]),
                                 (xnT_h[:, n % 2, k, :], xnT_l[:, n % 2, k, :]), k == 0, k == EC - 1)
                last.then_inc(kvT_done, 1)

            def turn_kv(r, n):
                pe.wait_ge(kvT_ready, upto(r, n + 1))
                for t in range(TILES):
                    cols = slice(t * P, (t + 1) * P)
                    last = nc.tensor.transpose(kv_bank(r, n)[:, cols], kvT[:, cols], ident[:, :])
                last.then_inc(kv_turned, 1)

            def project_q(r, n):
                if isinstance(r, int) and n < 3:
                    pe.wait_ge(xnT_ready, n + 1)
                    pe.wait_ge(wqq_ready, 1)
                    if n == 2:
                        pe.wait_ge(x1_ready, 1)
                else:
                    pe.wait_ge(x2T_ready, upto(r, n - 1))
                for k in range(EC):
                    last = three(q_bank(r, n)[:, :], (wqq_h[:, k, :], wqq_l[:, k, :]),
                                 (xnT_h[:, n % 2, k, :], xnT_l[:, n % 2, k, :]), k == 0, k == EC - 1)
                last.then_inc(q_done, 1)

            def energy_sum(r, n):
                pe.wait_ge(kv_ready, upto(r, n + 1))
                if not closes_batch(n):
                    if there(r, n - PER_BATCH):
                        pe.wait_ge(eo_ready, upto_batches(r, n))
                for t in range(TILES):
                    flat = [kv[:, t, s, :, :].rearrange("p h d -> p (h d)") for s in range(2)]
                    last = mm(e_ps[:, 0:P], flat[1], flat[0], start=(t == 0 and not closes_batch(n)),
                              stop=(t == TILES - 1 and closes_batch(n)))
                last.then_inc(energy_done, 1)

            def energy_times_wo(r, n):
                pe.wait_ge(energy_ready, upto_batches(r, n + 1))
                if isinstance(r, int) and n == PER_BATCH - 1:
                    pe.wait_ge(w_loaded["o"], 16)
                mm(e_ps[:, 0:EMB], energy[:, :, :].rearrange("p t d -> p (t d)"), wo2[:, :],
                   start=True, stop=True).then_inc(eo_done, 1)

            def attend(r, n):
                pe.wait_ge(eo_ready, upto_batches(r, n + PER_BATCH))
                pe.wait_ge(q_ready, upto(r, n + 2 if there(r, n + 1) else n + 1))
                for t in range(TILES):
                    dst = work_ps[t // 2][:, (t % 2) * EMB:(t % 2 + 1) * EMB]
                    q = qT[:, n % 2, t * P:(t + 1) * P]
                    mm(dst, q, eo_h[:, :], start=True, stop=False)
                    last = mm(dst, q, eo_l[:, :], start=False, stop=True)
                last.then_inc(att_done, 1)

            def project_up(r, i, c):
                if c == 0:
                    pe.wait_ge(x2T_ready, upto(r, i + 1))
                    if isinstance(r, int) and i == 0:
                        pe.wait_ge(wup_ready, 2)
                if there(r, i - 1) or c > 1:
                    pe.wait_ge(relu_done, upto(r, i, FC, c - 1))
                for k in range(EC):
                    cols = slice(c * P, (c + 1) * P)
                    last = three(hid_ps[c % 2][:, :], (wup_h[:, k, cols], wup_l[:, k, cols]),
                                 (x2T_h[:, i % 2, k, :], x2T_l[:, i % 2, k, :]), k == 0, k == EC - 1)
                last.then_inc(up_done, 1)

            def project_down(r, n, c):
                t, half = c // 2, c % 2
                if isinstance(r, int) and n == 0 and c == 0:
                    pe.wait_ge(wdn_ready, 2)
                if c < 2:
                    pe.wait_ge(hid_ready, upto(r, n, FC, (c + 1) * FC // 2))
                if c % 4 == 0:
                    pe.wait_ge(y_free, upto(r, n, 2, t // 2 + 1))
                dst = y_ps[t // 2][:, (t % 2) * EMB:(t % 2 + 1) * EMB]
                cols = slice(t * P, (t + 1) * P)
                for f in range(half * FC // 2, (half + 1) * FC // 2):
                    last = three(dst, (hid_h[:, n % 2, f, cols], hid_l[:, n % 2, f, cols]),
                                 (wdn_h[:, f, :], wdn_l[:, f, :]), f == 0, f == FC - 1)
                if c % 4 == 3:
                    last.then_inc(y_done, 1)

            def last_project_down(t, halves):
                cols = slice(t * P, (t + 1) * P)
                for half in halves:
                    pe.wait_ge(hid_ready, (GROUPS - 1) * FC + (half + 1) * FC // 2)
                    for f in range(half * FC // 2, (half + 1) * FC // 2):
                        last = three(last_banks[t][:, 0:EMB], (hid_h[:, (GROUPS - 1) % 2, f, cols],
                                                               hid_l[:, (GROUPS - 1) % 2, f, cols]),
                                     (wdn_h[:, f, :], wdn_l[:, f, :]), f == 0, f == FC - 1)
                if 1 in halves:
                    last.then_inc(last_y_done, 1)

            def step(r, i):
                if is_last(r, i - 1):
                    last_project_down(0, [0])
                    last_project_down(1, [0])
                    last_project_down(0, [1])
                    last_project_down(1, [1])
                    last_project_down(2, [0, 1])
                    last_project_down(3, [0, 1])
                    return
                for c in range(FC):
                    if there(r, i):
                        project_up(r, i, c)
                    if there(r, i - 1):
                        project_down(r, i - 1, c)
                    if c == 0 and there(r, i + 2) and not is_first(r, i):
                        project_q(r, i + 2)
                    if c == 1 and there(r, i + 2) and not is_first(r, i):
                        energy_sum(r, i + 2)
                    if c == 2 and there(r, i + 2) and closes_batch(i + 2):
                        energy_times_wo(r, i + 2)
                    if c == 3 and there(r, i + 1):
                        attend(r, i + 1)
                    if c == 4 and there(r, i + 3):
                        turn_first(r, i + 3)
                    if c == 6 and there(r, i + 3):
                        project_kv(r, i + 3)
                    if c == 6 and there(r, i + 1):
                        turn_second(r, i + 1)
                    if c == 7 and there(r, i + 3):
                        turn_kv(r, i + 3)

            keep_warm(9)
            turn_first(0, 0)
            turn_first(0, 1)
            keep_warm(1)
            project_kv(0, 0)
            project_kv(0, 1)
            turn_kv(0, 0)
            project_q(0, 0)
            turn_kv(0, 1)
            energy_sum(0, 0)
            project_q(0, 1)
            energy_sum(0, 1)
            turn_first(0, 2)
            energy_times_wo(0, PER_BATCH - 1)
            keep_warm(1)
            attend(0, 0)
            project_kv(0, 2)
            project_q(0, 2)
            turn_kv(0, 2)
            keep_warm(3)
            turn_second(0, 0)
            energy_sum(0, 2)
            keep_warm(3, work_ps[1])
            steps(pe, step)


def kernel(L0_attn_x, L0_attn_wq, L0_attn_wk, L0_attn_wv, L0_attn_wo, L0_ffn_W_fc, L0_ffn_W_proj):
    import concourse.bacc as bacc
    from concourse.bass_utils import run_bass_kernel_spmd

    def chunks(w):
        rows, n = w.shape
        return np.ascontiguousarray(w.reshape(rows // P, P, n).transpose(1, 0, 2).reshape(P, -1))

    x, wq, wk, wv, wo, w_fc, w_proj = (np.asarray(a) for a in (
        L0_attn_x, L0_attn_wq, L0_attn_wk, L0_attn_wv, L0_attn_wo, L0_ffn_W_fc, L0_ffn_W_proj))
    arrays = {
        "x": np.ascontiguousarray(x.reshape(-1, EMB)),
        "w_kv": chunks(np.concatenate([wk.T, wv.T], axis=1)),
        "w_qq": chunks(np.concatenate([wq.T, wq.T], axis=1)),
        "w_o": np.concatenate([wo.T, wo.T], axis=0),
        "w_up": chunks(w_fc.T),
        "w_down": chunks(w_proj.T),
    }
    nc = bacc.Bacc("TRN2", target_bir_lowering=False, num_devices=1)
    args = [nc.dram_tensor(f"{n}_dram", a.shape, mybir.dt.float32, kind="ExternalInput").ap()
            for n, a in arrays.items()]
    out = nc.dram_tensor("out_dram", (BATCHES * SEQ, EMB), mybir.dt.float32, kind="ExternalOutput").ap()
    build(nc, *args, out)
    r = run_bass_kernel_spmd(nc, [{f"{n}_dram": a for n, a in arrays.items()}], core_ids=[0])
    return r.results[0]["out_dram"].reshape(BATCHES, SEQ, EMB)
```
